# Optimizing a Trainium2 kernel written in Bass

```python
import numpy as np
import jax
import jax.numpy as jnp

def _softmax(x, axis=-1):
    return jax.nn.softmax(x, axis=axis)

def _gelu(x):
    return jax.nn.gelu(x, approximate=True)

def _silu(x):
    return jax.nn.silu(x)

def _sigmoid(x):
    return jax.nn.sigmoid(x)

def _layernorm(x, axis=-1, eps=1e-05):
    m = jnp.mean(x, axis=axis, keepdims=True)
    v = jnp.var(x, axis=axis, keepdims=True)
    return (x - m) / jnp.sqrt(v + eps)

def _scatter_add(tgt, idx, src, axis=0):
    return tgt.at[idx].add(src)

def _segment_sum(src, seg, n):
    return jax.ops.segment_sum(src, seg, n)
kernel_name = 'mk_recurrent_d2_jaxref_r8_8f3f67'

def setup_inputs(seed: int=0):
    np.random.seed(seed)
    _w = jnp.asarray

    def _L0_attn_setup():
        import jax, jax.numpy as jnp
        import numpy as np

        def _sin_rpe(Lq, d_model, dtype):
            inv_freq = 1.0 / 10000.0 ** (jnp.arange(0, d_model, 2, dtype=jnp.float32) / d_model)
            pos = jnp.arange(-(Lq - 1), Lq, dtype=jnp.float32)
            ang = pos[:, None] * inv_freq[None, :]
            emb = jnp.zeros((2 * Lq - 1, d_model), dtype=jnp.float32)
            emb = emb.at[:, 0::2].set(jnp.sin(ang)).at[:, 1::2].set(jnp.cos(ang))
            return emb.astype(dtype)

        def _rel_shift(x):
            B, H, Lq, Lr = x.shape
            xp = jnp.concatenate([jnp.zeros((B, H, Lq, 1), x.dtype), x], axis=-1)
            xp = xp.reshape(B, H, Lr + 1, Lq)
            return xp[:, :, 1:].reshape(B, H, Lq, Lr)[..., Lr - Lq:]
        key = jax.random.key(seed)
        ks = jax.random.split(key, 7)
        B, Lq, D, H = (1, 256, 128, 16)
        d_head = D // H
        s = 0.02
        return {'w': jax.random.normal(ks[0], (B, Lq, D), jnp.float32), 'Wq': jax.random.normal(ks[1], (D, D), jnp.float32) * s, 'Wk': jax.random.normal(ks[2], (D, D), jnp.float32) * s, 'Wv': jax.random.normal(ks[3], (D, D), jnp.float32) * s, 'Wr': jax.random.normal(ks[4], (D, D), jnp.float32) * s, 'u_bias': jax.random.normal(ks[5], (H, d_head), jnp.float32) * 0.02, 'v_bias': jax.random.normal(ks[6], (H, d_head), jnp.float32) * 0.02}
    _L0_attn_in = _L0_attn_setup()

    def _L0_ffn_setup():
        import jax, jax.numpy as jnp
        import numpy as np
        DIM = 128
        HIDDEN = 384
        SCALE = 1.0 / 127.0

        def _dequant(w_int, dtype):
            return w_int.astype(dtype) * jnp.asarray(SCALE, dtype)
        key = jax.random.key(seed)
        k_x, k_g, k_u, k_d = jax.random.split(key, 4)
        x = jax.random.normal(k_x, (4, 256, DIM), dtype=jnp.float32)
        w_gate = jax.random.randint(k_g, (HIDDEN, DIM), -127, 128, dtype=jnp.int32)
        w_up = jax.random.randint(k_u, (HIDDEN, DIM), -127, 128, dtype=jnp.int32)
        w_down = jax.random.randint(k_d, (DIM, HIDDEN), -127, 128, dtype=jnp.int32)
        return {'x': x, 'w_gate': w_gate, 'w_up': w_up, 'w_down': w_down}
    _L0_ffn_in = _L0_ffn_setup()

    def _L1_attn_setup():
        import jax, jax.numpy as jnp
        import numpy as np
        N, B, C = (36, 64, 128)
        H = 16
        P_PER_TASK = 4
        NUM_TASKS = 7

        def _prompt_mask(n, p, num_tasks, dtype):
            P = (num_tasks + 1) * p
            r = jnp.arange(n)[:, None]
            c = jnp.arange(n)[None, :]
            blocked = (c < P) & ~((r < P) & (r >= c // p * p))
            return jnp.where(blocked, -jnp.inf, 0.0).astype(dtype)
        key = jax.random.key(seed)
        k1, k2, k3 = jax.random.split(key, 3)
        x = jax.random.normal(k1, (N, B, C), dtype=jnp.float32)
        Wqkv = jax.random.normal(k2, (3 * C, C), dtype=jnp.float32) * 0.02
        bqkv = jnp.zeros((3 * C,), dtype=jnp.float32)
        Wproj = jax.random.normal(k3, (C, C), dtype=jnp.float32) * 0.02
        bproj = jnp.zeros((C,), dtype=jnp.float32)
        return {'x': x, 'Wqkv': Wqkv, 'bqkv': bqkv, 'Wproj': Wproj, 'bproj': bproj}
    _L1_attn_in = _L1_attn_setup()

    def _L1_ffn_setup():
        import jax, jax.numpy as jnp
        import numpy as np
        B, S, D, H, DOUT, E, K = (4, 256, 128, 128, 128, 8, 2)
        key = jax.random.key(seed)
        k1, k2, k3, k4 = jax.random.split(key, 4)
        x = jax.random.normal(k1, (B, S, D), dtype=jnp.float32)
        Wr = jax.random.normal(k2, (D, E), dtype=jnp.float32) * 0.02
        Wi = jax.random.normal(k3, (E, D, H), dtype=jnp.float32) * 0.02
        Wo = jax.random.normal(k4, (E, H, DOUT), dtype=jnp.float32) * 0.02
        return {'x': x, 'Wr': Wr, 'Wi': Wi, 'Wo': Wo}
    _L1_ffn_in = _L1_ffn_setup()
    _d = {'L0_attn_w': _L0_attn_in['w'], 'L0_attn_Wq': _L0_attn_in['Wq'], 'L0_attn_Wk': _L0_attn_in['Wk'], 'L0_attn_Wv': _L0_attn_in['Wv'], 'L0_attn_Wr': _L0_attn_in['Wr'], 'L0_attn_u_bias': _L0_attn_in['u_bias'], 'L0_attn_v_bias': _L0_attn_in['v_bias'], 'L0_ffn_w_gate': _L0_ffn_in['w_gate'], 'L0_ffn_w_up': _L0_ffn_in['w_up'], 'L0_ffn_w_down': _L0_ffn_in['w_down'], 'L1_attn_Wqkv': _L1_attn_in['Wqkv'], 'L1_attn_bqkv': _L1_attn_in['bqkv'], 'L1_attn_Wproj': _L1_attn_in['Wproj'], 'L1_attn_bproj': _L1_attn_in['bproj'], 'L1_ffn_Wr': _L1_ffn_in['Wr'], 'L1_ffn_Wi': _L1_ffn_in['Wi'], 'L1_ffn_Wo': _L1_ffn_in['Wo']}
    _x0 = _d['L0_attn_w']
    _d['L0_attn_w'] = jax.random.normal(jax.random.fold_in(jax.random.key(seed), 1), (4, 512, 128), dtype=_x0.dtype)
    del _x0
    return _d

def reference(L0_attn_w, L0_attn_Wq, L0_attn_Wk, L0_attn_Wv, L0_attn_Wr, L0_attn_u_bias, L0_attn_v_bias, L0_ffn_w_gate, L0_ffn_w_up, L0_ffn_w_down, L1_attn_Wqkv, L1_attn_bqkv, L1_attn_Wproj, L1_attn_bproj, L1_ffn_Wr, L1_ffn_Wi, L1_ffn_Wo):

    def _L0_attn_ref(w, Wq, Wk, Wv, Wr, u_bias, v_bias):
        import jax, jax.numpy as jnp
        import numpy as np

        def _sin_rpe(Lq, d_model, dtype):
            inv_freq = 1.0 / 10000.0 ** (jnp.arange(0, d_model, 2, dtype=jnp.float32) / d_model)
            pos = jnp.arange(-(Lq - 1), Lq, dtype=jnp.float32)
            ang = pos[:, None] * inv_freq[None, :]
            emb = jnp.zeros((2 * Lq - 1, d_model), dtype=jnp.float32)
            emb = emb.at[:, 0::2].set(jnp.sin(ang)).at[:, 1::2].set(jnp.cos(ang))
            return emb.astype(dtype)

        def _rel_shift(x):
            B, H, Lq, Lr = x.shape
            xp = jnp.concatenate([jnp.zeros((B, H, Lq, 1), x.dtype), x], axis=-1)
            xp = xp.reshape(B, H, Lr + 1, Lq)
            return xp[:, :, 1:].reshape(B, H, Lq, Lr)[..., Lr - Lq:]
        B, Lq, D = w.shape
        H, d_head = u_bias.shape
        scale = 1.0 / np.sqrt(d_head).astype(np.float32)
        r = _sin_rpe(Lq, D, w.dtype)
        q = (w @ Wq.T).reshape(B, Lq, H, d_head).transpose(0, 2, 1, 3)
        k = (w @ Wk.T).reshape(B, Lq, H, d_head).transpose(0, 2, 1, 3)
        v = (w @ Wv.T).reshape(B, Lq, H, d_head).transpose(0, 2, 1, 3)
        rp = (r @ Wr.T).reshape(2 * Lq - 1, H, d_head).transpose(1, 0, 2)
        AC = jnp.einsum('bhid,bhjd->bhij', q + u_bias[None, :, None, :], k)
        BD = jnp.einsum('bhid,hjd->bhij', q + v_bias[None, :, None, :], rp)
        BD = _rel_shift(BD)
        attn = jax.nn.softmax((AC + BD) * scale, axis=-1)
        out = jnp.einsum('bhij,bhjd->bhid', attn, v)
        return out.transpose(0, 2, 1, 3).reshape(B, Lq, D)

    def _L0_ffn_ref(x, w_gate, w_up, w_down):
        import jax, jax.numpy as jnp
        import numpy as np
        DIM = 128
        HIDDEN = 384
        SCALE = 1.0 / 127.0

        def _dequant(w_int, dtype):
            return w_int.astype(dtype) * jnp.asarray(SCALE, dtype)
        wg = _dequant(w_gate, x.dtype)
        wu = _dequant(w_up, x.dtype)
        wd = _dequant(w_down, x.dtype)
        gate = jnp.einsum('bsd,hd->bsh', x, wg)
        up = jnp.einsum('bsd,hd->bsh', x, wu)
        h = jax.nn.silu(gate) * up
        return jnp.einsum('bsh,dh->bsd', h, wd)

    def _L1_attn_ref(x, Wqkv, bqkv, Wproj, bproj):
        import jax, jax.numpy as jnp
        import numpy as np
        N, B, C = (36, 64, 128)
        H = 16
        P_PER_TASK = 4
        NUM_TASKS = 7

        def _prompt_mask(n, p, num_tasks, dtype):
            P = (num_tasks + 1) * p
            r = jnp.arange(n)[:, None]
            c = jnp.arange(n)[None, :]
            blocked = (c < P) & ~((r < P) & (r >= c // p * p))
            return jnp.where(blocked, -jnp.inf, 0.0).astype(dtype)
        n, b, ch = x.shape
        hd = ch // H
        scale = hd ** (-0.5)
        qkv = x @ Wqkv.T + bqkv
        q, k, v = jnp.split(qkv, 3, axis=-1)
        to_heads = lambda t: t.reshape(n, b * H, hd).transpose(1, 0, 2)
        q, k, v = (to_heads(q), to_heads(k), to_heads(v))
        mask = _prompt_mask(n, P_PER_TASK, NUM_TASKS, x.dtype)
        scores = mask + scale * jnp.einsum('bnd,bmd->bnm', q, k)
        attn = jax.nn.softmax(scores, axis=-1)
        out = jnp.einsum('bnm,bmd->bnd', attn, v)
        out = out.transpose(1, 0, 2).reshape(n, b, ch)
        return out @ Wproj.T + bproj

    def _L1_ffn_ref(x, Wr, Wi, Wo):
        import jax, jax.numpy as jnp
        import numpy as np
        B, S, D, H, DOUT, E, K = (4, 256, 128, 128, 128, 8, 2)
        b, s, d = x.shape
        e_cnt, _, h = Wi.shape
        dout = Wo.shape[2]
        xf = x.reshape(-1, d)
        T = xf.shape[0]
        probs = jax.nn.softmax(xf @ Wr, axis=-1)
        topk_p, topk_i = jax.lax.top_k(probs, K)
        mask = topk_i[:, :, None] == jnp.arange(e_cnt)[None, None, :]
        hmix = jnp.zeros((T, K, h), dtype=xf.dtype)
        for e in range(e_cnt):
            he = xf @ Wi[e]
            hmix = hmix + jnp.where(mask[:, :, e][:, :, None], he[:, None, :], 0.0)
        o = jnp.zeros((T, K, dout), dtype=xf.dtype)
        for e in range(e_cnt):
            oe = jnp.einsum('tkh,hd->tkd', hmix, Wo[e])
            o = o + jnp.where(mask[:, :, e][:, :, None], oe, 0.0)
        out = jnp.sum(o * topk_p[:, :, None], axis=1)
        return out.reshape(b, s, dout)
    x = L0_attn_w
    xn = _layernorm(x, axis=-1)
    s = _L0_attn_ref(xn, L0_attn_Wq, L0_attn_Wk, L0_attn_Wv, L0_attn_Wr, L0_attn_u_bias, L0_attn_v_bias)
    g = _silu(_L0_ffn_ref(xn, L0_ffn_w_gate, L0_ffn_w_up, L0_ffn_w_down))
    x = x + s * g
    xn = _layernorm(x, axis=-1)
    s = _L1_attn_ref(xn, L1_attn_Wqkv, L1_attn_bqkv, L1_attn_Wproj, L1_attn_bproj)
    g = _silu(_L1_ffn_ref(xn, L1_ffn_Wr, L1_ffn_Wi, L1_ffn_Wo))
    x = x + s * g
    return x

_drawn_inputs = setup_inputs


def setup_inputs(seed=0):
    import zlib

    import numpy as np

    out = dict(_drawn_inputs(seed))
    spreads = {'L1_attn_bqkv': (0.0, 0.8), 'L1_attn_bproj': (0.0, 0.8)}
    factors = {'L0_attn_u_bias': 4.915,
     'L0_attn_v_bias': 8.0,
     'L1_attn_Wqkv': 8.0,
     'L1_attn_Wproj': 8.0,
     'L1_ffn_Wr': 8.0,
     'L1_ffn_Wi': 8.0,
     'L1_ffn_Wo': 8.0}
    for name, (base, spread) in spreads.items():
        noise = np.random.default_rng([zlib.crc32(name.encode()), seed]).standard_normal(out[name].shape)
        drawn = base * np.exp(spread * noise) if base else spread * noise
        out[name] = jnp.asarray(drawn.astype(out[name].dtype))
    for name, factor in factors.items():
        out[name] = (out[name] * factor).astype(out[name].dtype)
    return out
```

```python
from contextlib import ExitStack

import numpy as np

import concourse.bass as bass
from concourse import mybir
from concourse.alu_op_type import AluOpType as ALU

ACT = mybir.ActivationFunctionType
AX = mybir.AxisListType
F32 = mybir.dt.float32
BF16 = mybir.dt.bfloat16
I32 = mybir.dt.int32

P = 128
NB, L, D = 4, 512, 128
H, DH = 16, 8
TPB = L // P
T = NB * TPB
HID = 384
E_CNT, TOPK = 8, 2
SCALE = 1.0 / float(np.sqrt(np.float32(DH)))
DEQ = 1.0 / 127.0
EPS = 1e-5
BIG = 1e30
SPLITS = 3
ROWS = SPLITS * SPLITS * DH
WIDE = L + P
WQ, WV, WK, WG, WU, WD, WI, WP, WQKV = 0, 1, 2, 3, 6, 9, 12, 20, 21
WBLOCKS = 24
QKVR = 3 * D + E_CNT


def tables():
    freq = (1.0 / 10000.0 ** (np.arange(0, D, 2, dtype=np.float64) / D)).astype(np.float32).astype(np.float64)
    f = np.repeat(freq, 2)[:, None]
    odd = (np.arange(D) % 2)[:, None]

    def waves(pos):
        return np.where(odd, np.cos(f * pos), np.sin(f * pos))

    key = np.arange(L, dtype=np.float64)[None, :]
    turn = f * (key - (L - 1))
    low = waves(key)
    up = waves(key - (2 * L - 1))
    cos_t = np.cos(turn)
    sin_t = np.where(odd, -np.sin(turn), np.sin(turn))
    rot = np.stack([np.concatenate([cos_t[:, c:c + L // 2], sin_t[:, c:c + L // 2]], 1) for c in (0, L // 2)], 1)
    mask = np.zeros((P, TPB, WIDE), np.float32)
    for tile in range(TPB):
        q = tile * P + np.arange(P)[:, None]
        k = np.arange(L)[None, :]
        bad = np.where(k < (tile + 1) * P, k > q, k < q + 2)
        mask[:, tile, :L][bad] = -BIG
        kd = tile * P + np.arange(P)[None, :]
        mask[:, tile, L:][kd < q + 2] = -BIG
    tri = np.tile((np.arange(E_CNT)[None, :] < np.arange(E_CNT)[:, None]).astype(np.float32).reshape(1, -1), (P, 1))
    last = np.zeros((P, T), np.float32)
    last[P - 1, TPB - 1::TPB] = BIG
    small = np.concatenate([np.eye(P, dtype=np.float32), tri, last], 1)
    return {
        "c_small": small,
        "c_waves": np.stack([low, up], 1).astype(np.float32),
        "c_rot": rot.astype(np.float32),
        "c_mask": mask,
    }


def build(nc, w, Wq, Wk, Wv, Wr, u_bias, v_bias, w_gate, w_up, w_down,
          Wqkv, bqkv, Wproj, bproj, Wr1, Wi, Wo, c_small, c_waves, c_rot, c_mask, out):
    ctx = ExitStack()
    with ctx:
        def sb(name, shape, dt=F32):
            return ctx.enter_context(nc.sbuf_tensor(name, shape, dt))

        def sem(name):
            return ctx.enter_context(nc.semaphore(name))

        qv_parts = nc.dram_tensor("qv_parts", (H, NB, SPLITS, DH, L), BF16, kind="Internal").ap()
        qu_parts = nc.dram_tensor("qu_parts", (H, NB, SPLITS, DH, L), BF16, kind="Internal").ap()
        k_parts = nc.dram_tensor("k_parts", (H, NB, 5, DH, L), BF16, kind="Internal").ap()
        wr_parts = nc.dram_tensor("wr_parts", (H, 5, DH, 2 * D), BF16, kind="Internal").ap()

        x = sb("x", [P, T, D])
        eps_col = sb("eps_col", [P, 1])
        xn = sb("xn", [P, T, D])
        xnT = sb("xnT", [P, NB * L + 1])
        stats = sb("stats", [P, T, 6])
        mean_var = sb("mean_var", [P, T, 2])
        rstd = sb("rstd", [P, T])
        w_nat = sb("w_nat", [P, WBLOCKS, D])
        w_int = sb("w_int", [P, 9, D], I32)
        wT = sb("wT", [P, WBLOCKS * D + E_CNT])
        wo1 = sb("wo1", [P, E_CNT, D])
        wr_nat = sb("wr_nat", [P, 2, D])
        wr_s = sb("wr_s", [P, SPLITS, 2 * D], BF16)
        small = sb("small", [P, P + E_CNT * E_CNT + T])
        ident = small[:, 0:P]
        tri = small[:, P:P + E_CNT * E_CNT]
        last_key = small[:, P + E_CNT * E_CNT:]
        waves = sb("waves", [P, 2, L])
        rot = sb("rot", [P, 2, L])
        mask = sb("mask", [P, TPB, WIDE])
        ub_col = sb("ub_col", [P, 1])
        vb_col = sb("vb_col", [P, 1])
        ub_row = sb("ub_row", [P, D])
        b_row = sb("b_row", [P, QKVR])
        bp_row = sb("bp_row", [P, D])
        arena = sb("arena", [P, 3 * NB * SPLITS * L // 2])
        parts = arena[:, :].bitcast(BF16).rearrange("p (a b s n) -> p a b s n", a=3, b=NB, s=SPLITS)
        qkv = arena[:, 0:T * QKVR].rearrange("p (t c) -> p t c", t=T)
        rest = sb("rest", [P, 2, L])
        vones = sb("vones", [P, T, H, DH + 1])
        v_next = sb("v_next", [P, T, D])
        neg_s = sb("neg_s", [P, H, T])
        shift = sb("shift", [P, H, T])
        ffn = sb("ffn", [P, T, D])
        o_all = sb("o_all", [P, T, H, DH + 1])
        qu_st = sb("qu_st", [ROWS, 2, L], BF16)
        qv_st = sb("qv_st", [ROWS, 2, L], BF16)
        k_st = sb("k_st", [ROWS, 2, L], BF16)
        wr_st = sb("wr_st", [ROWS, 2 * D], BF16)
        work = sb("work", [P, 7680])

        def area(at, *shape):
            n = int(np.prod(shape))
            names = "abcd"[:len(shape)]
            return work[:, at:at + n].rearrange(f"p ({' '.join(names)}) -> p {' '.join(names)}",
                                                **dict(zip(names, shape)))

        turned_g = area(0, 2, L)
        g_sb = area(1024, 2, L + 1)
        s_sb = area(2050, 2, WIDE)
        prob = area(3330, 2, WIDE)
        probT = area(4610, 2, L)
        peak = sb("peak", [P, 2])
        pace = sb("pace", [P, 2])

        bank = [ctx.enter_context(nc.psum_tensor(f"bank{i}", [P, 2, 512], F32)) for i in range(4)]

        def B(i):
            return bank[i // 2][:, i % 2, :]

        in_x = [sem(f"in_x{i}") for i in range(2)]
        in_w0, in_wint, in_w1, in_small, in_tab, in_bias, in_b1 = (
            sem(n) for n in ("in_w0", "in_wint", "in_w1", "in_small", "in_tab", "in_bias", "in_b1"))
        block = ctx.enter_context(nc.Block())

        S = {}

        def s_(name):
            if name not in S:
                S[name] = sem(name)
            return S[name]

        names = ["cast", "dve_self", "sd", "xn_ready", "turned_a", "evac_v", "evac_a", "proj", "part1", "part_done",
                 "scr", "wr_done", "init", "tok", "vt", "qk", "neg", "gu", "th", "hT", "down", "th2", "ffn_ready",
                 "g_done", "g_rot", "g_ready", "scored", "maxed", "shifted", "exped", "merged", "turned", "evaced",
                 "pvd", "o_evac", "e1_in", "e1", "x2_ready", "sd2", "xn2", "turned_b", "evac_b", "qkvd", "qkvb",
                 "wcd", "wcb", "moed", "moes", "lmax", "lexp", "pmax", "pexp", "attn", "attnT", "attnTs", "pj",
                 "res", "gth", "fin", "stored"]
        for n in names:
            s_(n)
        ld = [sem(f"ld{i}") for i in range(2)]
        ldqv = [sem(f"ldqv{i}") for i in range(2)]
        ld_wr = sem("ld_wr")

        xr = w.rearrange("b (i p) c -> p (b i) c", p=P)
        outr = out.rearrange("b (i p) c -> p (b i) c", p=P)
        fills_a = [(0, "w", 0)] + [(i, "x", i - 1) for i in range(1, 5)] + [(i, "w", i - 4) for i in range(5, 10)]
        dve_fills = [f for f, _, _ in fills_a if f % 2 == 1]
        act_fills = [f for f, _, _ in fills_a if f % 2 == 0]

        def after_a(eng, f):
            if f % 2:
                eng.wait_ge(S["evac_v"], dve_fills.index(f) + 1)
            else:
                eng.wait_ge(S["evac_a"], act_fills.index(f) + 1)

        prod0 = area(0, T, D)
        tq = area(2048, 2, D)
        s_next = work[:, 2304:2560]
        th = area(2560, 3, L)
        hg = area(4096, 2, L)
        hTt = area(5120, 3, L)
        th2 = area(6656, 2, L)
        e1d = work[:, 0:H * T]
        e1 = work[:, 256:256 + H * T]
        num = area(512, 2, L)
        den = area(1536, 2, TPB * H)
        prod1 = area(2048, 2048)
        sc = area(4096, NB, NB, TPB * H)
        pr = area(5120, NB, NB, TPB * H)
        smax = area(6144, NB, TPB * H)
        ssum = area(6400, NB, TPB * H)
        gate = area(6656, T, E_CNT)
        rank = area(6784, T, E_CNT)
        rsum = area(6912, T)
        lg = area(6928, T, E_CNT)
        gt = area(2048, T, E_CNT * E_CNT)
        eq = area(3072, T, E_CNT * E_CNT)
        moe_tmp = area(2048, 2, E_CNT * D)
        attn = v_next
        attnT = ffn[:, :, :].rearrange("p t c -> p (t c)")
        moe = xn
        th_moe = o_all[:, :, :, :].rearrange("p t h d -> p (t h d)")[:, 0:T * D].rearrange("p (n c) -> p n c", n=NB)
        wc = w_nat[:, 0:E_CNT, :]

        @block.sync
        def _(sp):
            sp.dma_start(x[:, 0:8, :], xr[:, 0:8, :]).then_inc(in_x[0], 16)
            sp.dma_start(w_nat[:, WQ, :], Wq).then_inc(in_w0, 16)
            sp.dma_start(w_nat[:, WV, :], Wv).then_inc(in_w0, 16)
            sp.dma_start(w_nat[:, WK, :], Wk).then_inc(in_w0, 16)
            sp.dma_start(wr_nat[:, 0, :], Wr).then_inc(in_w0, 16)
            sp.dma_start(x[:, 8:16, :], xr[:, 8:16, :]).then_inc(in_x[1], 16)
            sp.dma_start(waves[:, :, :], c_waves).then_inc(in_tab, 16)
            sp.dma_start(rot[:, :, :], c_rot).then_inc(in_tab, 16)
            sp.dma_start(mask[:, :, :], c_mask).then_inc(in_tab, 16)
            sp.dma_start(w_nat[:, WI:WI + E_CNT, :], Wi.rearrange("e d h -> d e h")).then_inc(in_w1, 16)
            sp.dma_start(w_nat[:, WP, :], Wproj).then_inc(in_w1, 16)
            sp.dma_start(w_nat[:, WQKV:WQKV + 3, :], Wqkv.rearrange("(k p) c -> p k c", p=P)).then_inc(in_w1, 16)
            sp.dma_start(wT[:, WBLOCKS * D:], Wr1).then_inc(in_w1, 16)
            sp.dma_start(wo1[:, :, :], Wo.rearrange("e h d -> h e d")).then_inc(in_w1, 16)

            def piece(scr, h, b, lo, hi):
                at = scr[h:h + 1, b] if isinstance(h, int) else scr[bass.ds(h, 1), b]
                return at[:, lo:hi].rearrange("a s d n -> (a s d) n")

            def load_qv(h, b, base):
                if base is not None:
                    sp.wait_ge(S["g_done"], base)
                for r in range(SPLITS):
                    rows = slice(r * SPLITS * DH, (r + 1) * SPLITS * DH)
                    sp.dma_start(qv_st[rows, b % 2, :], piece(qv_parts, h, b, 0, 3)).then_inc(ldqv[b % 2], 16)

            def load_quk(h, b, base):
                if base is not None:
                    sp.wait_ge(S["scored"], base)
                for r in range(SPLITS):
                    rows = slice(r * SPLITS * DH, (r + 1) * SPLITS * DH)
                    sp.dma_start(qu_st[rows, b % 2, :], piece(qu_parts, h, b, 0, 3)).then_inc(ld[b % 2], 16)
                    sp.dma_start(k_st[rows, b % 2, :], piece(k_parts, h, b, r, r + 3)).then_inc(ld[b % 2], 16)

            def load_wr(h, base):
                if base is not None:
                    sp.wait_ge(S["g_done"], base)
                at = wr_parts[h:h + 1] if isinstance(h, int) else wr_parts[bass.ds(h, 1)]
                for r in range(SPLITS):
                    rows = slice(r * SPLITS * DH, (r + 1) * SPLITS * DH)
                    sp.dma_start(wr_st[rows, :], at[:, r:r + 3].rearrange("a s d n -> (a s d) n")).then_inc(ld_wr, 16)

            sp.wait_ge(S["wr_done"], 16 * 5)
            load_wr(0, None)
            sp.wait_ge(S["scr"], 16 * NB * 11)
            for b in range(NB):
                load_qv(0, b, 2 * (b - 1) if b >= 2 else None)
                if b >= 1:
                    load_quk(0, b - 1, 4 * (b - 2) if b >= 3 else None)
            with sp.Fori(1, H) as h:
                for b in range(NB):
                    if b == 0:
                        load_wr(h, h * 8)
                    load_qv(h, b, h * 8 + 2 * (b - 1))
                    if b == 0:
                        load_quk(h - 1, NB - 1, h * 16 - 8)
                    else:
                        load_quk(h, b - 1, h * 16 + 4 * (b - 2))
            load_quk(H - 1, NB - 1, H * 16 - 8)
            sp.wait_ge(S["fin"], NB)
            sp.dma_start(outr, x[:, :, :]).then_inc(S["stored"], 16)
            sp.wait_ge(S["stored"], 16)

        @block.gpsimd
        def _(pool):
            pool.memset(eps_col[:, :], EPS).then_inc(S["init"], 1)
            pool.memset(b_row[:, 3 * D:], 0.0).then_inc(S["init"], 1)
            pool.memset(xnT[:, NB * L:], 0.0).then_inc(S["init"], 1)
            pool.memset(vones[:, :, :, DH:], 1.0).then_inc(S["init"], 1)
            pool.dma_start(small[:, :], c_small).then_inc(in_small, 16)
            pool.dma_start(w_int[:, 0:3, :], w_gate.rearrange("(k p) c -> p k c", p=P)).then_inc(in_wint, 16)
            pool.dma_start(w_int[:, 3:6, :], w_up.rearrange("(k p) c -> p k c", p=P)).then_inc(in_wint, 16)
            pool.dma_start(w_int[:, 6:9, :], w_down.rearrange("d (k h) -> d k h", k=3)).then_inc(in_wint, 16)
            pool.dma_start(ub_col[:, :], u_bias.rearrange("h (d o) -> (h d) o", o=1)).then_inc(in_bias, 16)
            pool.dma_start(vb_col[:, :], v_bias.rearrange("h (d o) -> (h d) o", o=1)).then_inc(in_bias, 16)
            pool.dma_start(ub_row[:, :], u_bias.rearrange("h d -> (h d)").partition_broadcast(P)).then_inc(in_bias, 16)
            pool.dma_start(b_row[:, 0:3 * D], bqkv.partition_broadcast(P)).then_inc(in_b1, 16)
            pool.dma_start(bp_row[:, :], bproj.partition_broadcast(P)).then_inc(in_b1, 16)
            pool.wait_ge(S["part_done"], 1)
            for s in range(5):
                pool.dma_start(wr_parts[:, s], wr_s[:, s % 3, :]).then_inc(S["wr_done"], 16)
            for b in range(NB):
                for kind, (scr, n) in enumerate(((qv_parts, 3), (qu_parts, 3), (k_parts, 5))):
                    pool.wait_ge(S["part_done"], 2 + 3 * b + kind)
                    for s in range(n):
                        pool.dma_start(scr[:, b, s], parts[:, kind, b, s % 3, :]).then_inc(S["scr"], 16)

            def rotate(n, par, half, free):
                pool.wait_ge(S["g_rot"], n + 1)
                if free is not None:
                    pool.wait_ge(S["scored"], free)
                cols = slice(half * 256, half * 256 + 256)
                pool.tensor_tensor(g_sb[:, par, cols], turned_g[:, half, 0:256], turned_g[:, half, 256:512],
                                   ALU.add).then_inc(S["g_ready"], 1)

            def merge(U, i):
                pool.wait_ge(S["exped"], U + 1)
                cols = slice(i * P, i * P + P)
                par = i % 2
                pool.tensor_tensor(prob[:, par, cols], prob[:, par, cols], prob[:, par, L:WIDE],
                                   ALU.add).then_inc(S["merged"], 1)

            def head(h, first, last):
                for b in range(NB):
                    for i in range(TPB):
                        if i in (1, 2) and not (last and b == NB - 1):
                            half = i - 1
                            n = h * 8 + 2 * (b + 1) + half
                            free = None if first and b == 0 else h * 16 + 4 * b
                            rotate(n, (b + 1) % 2, half, free)
                        merge(h * 16 + 4 * b + i, i)

            pool.wait_ge(S["ffn_ready"], NB)
            pool.memset(g_sb[:, :, L:], 0.0).then_inc(S["init"], 1)
            rotate(0, 0, 0, None)
            rotate(1, 0, 1, None)
            head(0, True, False)
            with pool.Fori(1, H - 1) as h:
                head(h, False, False)
            head(H - 1, False, True)

        @block.scalar
        def _(act):
            act.wait_ge(S["dve_self"], 2 * T)
            act.wait_ge(S["init"], 4)
            act.activation(rstd[:, :], mean_var[:, :, 1], ACT.Sqrt, bias=eps_col[:, 0:1]).then_inc(S["sd"], 1)
            for f, what, n in fills_a:
                if f % 2 == 0:
                    act.wait_ge(S["turned_a"], f + 1)
                    dst = wT[:, n * 512:(n + 1) * 512] if what == "w" else xnT[:, n * 512:(n + 1) * 512]
                    act.activation(dst, B(f % 8), ACT.Copy).then_inc(S["evac_a"], 1)
            act.wait_ge(in_w0, 64)
            act.wait_ge(S["cast"], 5)
            act.activation(wr_s[:, 0, :], wr_nat[:, :, :], ACT.Copy).then_inc(S["part1"], 1)
            act.wait_ge(in_bias, 48)
            for b in range(NB):
                for kind in range(3):
                    act.wait_ge(S["proj"], 2 * b + (1 if kind < 2 else 2))
                    src = B(2 * b + (kind == 2))
                    if kind < 2:
                        act.activation(parts[:, kind, b, 0, :], src, ACT.Identity,
                                       bias=(vb_col, ub_col)[kind][:, 0:1]).then_inc(S["part1"], 1)
                    else:
                        act.activation(parts[:, kind, b, 0, :], src, ACT.Copy).then_inc(S["part1"], 1)
            act.wait_ge(S["init"], 4)
            for t in range(T):
                act.wait_ge(S["tok"], t + 1)
                act.activation(vones[:, t, :, 0:DH], B(t % 8)[:, 128:256].rearrange("p (h d) -> p h d", h=H),
                               ACT.Copy).then_inc(S["vt"], 1)
                act.activation(v_next[:, t, :], B(t % 8)[:, 256:384], ACT.Copy).then_inc(S["vt"], 1)
            for b in range(NB):
                for k in range(3):
                    j = 3 * b + k
                    act.wait_ge(S["gu"], j + 1)
                    if j >= 3:
                        act.wait_ge(S["hT"], j - 2)
                    act.activation(th[:, j % 3, :], B(2 * k), ACT.Tanh, scale=DEQ / 2).then_inc(S["th"], 1)
                act.wait_ge(S["down"], b + 1)
                if b >= 2:
                    act.wait_ge(S["ffn_ready"], b - 1)
                act.activation(th2[:, b % 2, :], B(6 + b % 2), ACT.Tanh, scale=DEQ ** 3 / 4).then_inc(S["th2"], 1)

            def evacuate(U, par, first):
                act.wait_ge(S["turned"], U + 1)
                if not first:
                    act.wait_ge(S["pvd"], U - 1)
                act.activation(probT[:, par, :], B(4 + par), ACT.Copy).then_inc(S["evaced"], 1)

            def head(h, first):
                for b in range(NB):
                    for i in range(TPB):
                        u = 4 * b + i
                        U = h * 16 + u
                        par = u % 2
                        act.wait_ge(S["shifted"], U + 1)
                        if not (first and u < 2):
                            act.wait_ge(S["turned"], U - 1)
                        bias = shift[:, h, u:u + 1] if isinstance(h, int) else shift[:, bass.ds(h, 1), u:u + 1]
                        act.activation(prob[:, par, :], s_sb[:, par, :], ACT.Exp, bias=bias,
                                       scale=SCALE).then_inc(S["exped"], 1)
                        if not (first and u < 2):
                            evacuate(U - 2, par, first and u < 4)

            head(0, True)
            with act.Fori(1, H) as h:
                head(h, False)
            evacuate(H * 16 - 2, 0, False)
            evacuate(H * 16 - 1, 1, False)
            act.wait_ge(S["e1_in"], 1)
            act.activation(e1, e1d, ACT.Exp).then_inc(S["e1"], 1)
            act.wait_ge(S["x2_ready"], T)
            act.activation(rstd[:, :], mean_var[:, :, 1], ACT.Sqrt, bias=eps_col[:, 0:1]).then_inc(S["sd2"], 1)
            for n in range(NB):
                act.wait_ge(S["turned_b"], n + 1)
                act.activation(xnT[:, n * L:(n + 1) * L], B(n), ACT.Copy).then_inc(S["evac_b"], 1)
            for n in range(2):
                act.wait_ge(S["wcd"], n + 1)
                act.activation(wc[:, 4 * n:4 * n + 4, :].rearrange("p e c -> p (e c)"), B(n), ACT.Copy).then_inc(S["wcb"], 1)
            act.wait_ge(S["lmax"], 1)
            act.activation(lg, lg, ACT.Exp).then_inc(S["lexp"], 1)
            act.wait_ge(S["pmax"], 1)
            act.activation(pr, sc, ACT.Exp, scale=SCALE).then_inc(S["pexp"], 1)
            for n in range(NB):
                act.wait_ge(S["attnT"], n + 1)
                act.activation(attnT[:, n * L:(n + 1) * L], B(n % 2), ACT.Copy).then_inc(S["attnTs"], 1)
            for n in range(NB):
                act.wait_ge(S["moes"], 4 * n + 4)
                act.activation(th_moe[:, n, :], moe[:, 4 * n:4 * n + 4, :].rearrange("p t c -> p (t c)"), ACT.Tanh,
                               scale=0.5).then_inc(S["gth"], 1)

        @block.vector
        def _(dve):
            for half in range(2):
                dve.wait_ge(in_x[half], 16)
                for t in range(8 * half, 8 * half + 8):
                    dve.bn_stats(stats[:, t, :], x[:, t, :]).then_inc(S["dve_self"], 1)
            for t in range(T):
                dve.wait_ge(S["dve_self"], T)
                dve.bn_aggr(mean_var[:, t, :], stats[:, t, :]).then_inc(S["dve_self"], 1)
            dve.wait_ge(in_wint, 48)
            for k in range(3):
                dve.tensor_copy(w_nat[:, WG + 3 * k:WG + 3 * k + 3, :], w_int[:, 3 * k:3 * k + 3, :]).then_inc(S["cast"], 1)
            dve.wait_ge(in_w0, 64)
            pair = wr_nat[:, 0, :].rearrange("p (k two) -> p k two", two=2)
            swap = wr_nat[:, 1, :].rearrange("p (k two) -> p k two", two=2)
            dve.tensor_copy(swap[:, :, 0], pair[:, :, 1]).then_inc(S["cast"], 1)
            dve.tensor_copy(swap[:, :, 1], pair[:, :, 0]).then_inc(S["cast"], 1)
            dve.wait_ge(S["sd"], 1)
            dve.reciprocal(rstd[:, :], rstd[:, :]).then_inc(S["dve_self"], 1)
            dve.wait_ge(S["dve_self"], 2 * T + 1)
            for t in range(T):
                dve.tensor_scalar(xn[:, t, :], x[:, t, :], mean_var[:, t, 0:1], rstd[:, t:t + 1],
                                  ALU.subtract, ALU.mult).then_inc(S["xn_ready"], 1)
            for f, what, n in fills_a:
                if f % 2 == 1:
                    dve.wait_ge(S["turned_a"], f + 1)
                    dst = wT[:, n * 512:(n + 1) * 512] if what == "w" else xnT[:, n * 512:(n + 1) * 512]
                    dve.tensor_copy(dst, B(f % 8)).then_inc(S["evac_v"], 1)
            c = [0]

            def link(ins):
                c[0] += 1
                ins.then_inc(S["qk"], 1)
                dve.wait_ge(S["qk"], c[0])

            dve.wait_ge(S["part1"], 1)
            r = rest[:, 0, 0:2 * D]
            link(dve.tensor_tensor(r, wr_nat[:, :, :].rearrange("p a c -> p (a c)"), wr_s[:, 0, :], ALU.subtract))
            link(dve.tensor_copy(wr_s[:, 1, :], r))
            dve.tensor_tensor(wr_s[:, 2, :], r, wr_s[:, 1, :], ALU.subtract).then_inc(S["part_done"], 1)
            dve.wait_ge(in_bias, 48)
            for b in range(NB):
                for kind in range(3):
                    n = 1 + 3 * b + kind
                    dve.wait_ge(S["part1"], n + 2 if kind == 0 else n + 1)
                    r = rest[:, n % 2, :]
                    src = B(2 * b + (kind == 2))
                    s1, s2, s3 = (parts[:, kind, b, s, :] for s in range(3))
                    if n >= 2:
                        dve.wait_ge(S["part_done"], n - 1)
                    if kind < 2:
                        link(dve.scalar_tensor_tensor(out=r, in0=src, scalar=(vb_col, ub_col)[kind][:, 0:1], in1=s1,
                                                      op0=ALU.add, op1=ALU.subtract))
                    else:
                        link(dve.tensor_tensor(r, src, s1, ALU.subtract))
                    link(dve.tensor_copy(s2, r))
                    dve.tensor_tensor(s3, r, s2, ALU.subtract).then_inc(S["part_done"], 1)
            for t in range(T):
                dve.wait_ge(S["vt"], 2 * t + 2)
                link(dve.tensor_tensor(tq[:, t % 2, :], B(t % 8)[:, 0:128], ub_row[:, :], ALU.add))
                dve.tensor_tensor(prod0[:, t, :], B(t % 8)[:, 384:512], tq[:, t % 2, :], ALU.mult).then_inc(S["neg"], 1)
            dve.wait_ge(S["neg"], T)
            link(dve.tensor_reduce(s_next, prod0.rearrange("p t (h d) -> p (t h) d", d=DH), AX.X, ALU.add))
            dve.wait_ge(in_small, 16)
            link(dve.tensor_scalar(s_next, s_next, -SCALE, None, ALU.mult))
            link(dve.tensor_tensor(neg_s[:, :, :].rearrange("p h t -> p t h"),
                                   s_next.rearrange("p (t h) -> p t h", h=H),
                                   last_key.unsqueeze(2).to_broadcast([P, T, H]), ALU.add))
            for b in range(NB):
                for k in range(3):
                    j = 3 * b + k
                    dve.wait_ge(S["th"], j + 1)
                    link(dve.scalar_tensor_tensor(out=hg[:, j % 2, :], in0=th[:, j % 3, :], scalar=1.0, in1=B(2 * k),
                                                  op0=ALU.add, op1=ALU.mult))
                    if b >= 1:
                        dve.wait_ge(S["down"], b)
                    dve.tensor_tensor(hTt[:, k, :], B(2 * k + 1), hg[:, j % 2, :], ALU.mult).then_inc(S["hT"], 1)
                dve.wait_ge(S["th2"], b + 1)
                dve.scalar_tensor_tensor(out=ffn[:, 4 * b:4 * b + 4, :].rearrange("p t c -> p (t c)"), in0=th2[:, b % 2, :],
                                         scalar=1.0, in1=B(6 + b % 2), op0=ALU.add, op1=ALU.mult).then_inc(S["ffn_ready"], 1)

            def rotate(n, half, first):
                dve.wait_ge(S["g_done"], n + 1)
                if not first:
                    dve.wait_ge(S["g_ready"], n - 1)
                dve.tensor_tensor(turned_g[:, half, :], B(6), rot[:, half, :], ALU.mult).then_inc(S["g_rot"], 1)

            def o_evacuate(h, b, n):
                dve.wait_ge(S["pvd"], 4 * n + 4)
                dst = o_all[:, 4 * b:4 * b + 4, h, :] if isinstance(h, int) else o_all[:, 4 * b:4 * b + 4, bass.ds(h, 1), :]
                src = B(7)[:, 0:4 * (DH + 1)].rearrange("p (i d) -> p i d", i=4)
                if not isinstance(h, int):
                    dst = dst.rearrange("p i a d -> p i (a d)")
                dve.tensor_copy(dst, src).then_inc(S["o_evac"], 1)

            def head(h, first, last):
                for b in range(NB):
                    for i in range(TPB):
                        u = 4 * b + i
                        U = h * 16 + u
                        par = u % 2
                        if i in (1, 2) and not (last and b == NB - 1):
                            rotate(h * 8 + 2 * (b + 1) + i - 1, i - 1, False)
                        if i == 3 and not (first and b == 0):
                            if b:
                                o_evacuate(h, b - 1, h * 4 + b - 1)
                            else:
                                o_evacuate(h - 1, NB - 1, h * 4 - 1)
                        dve.wait_ge(S["scored"], U + 1)
                        if not (first and u < 2):
                            dve.wait_ge(S["exped"], U - 1)
                        dve.memset(pace[:, par:par + 1], 0.0)
                        dve.tensor_tensor_reduce(s_sb[:, par, :], bank[par][:, :, :].rearrange("p a c -> p (a c)")[:, 0:WIDE],
                                                 mask[:, i, :], 1.0, -3e38, ALU.add, ALU.max,
                                                 peak[:, par:par + 1]).then_inc(S["maxed"], 1)
                        dve.wait_ge(S["maxed"], U + 1)
                        if isinstance(h, int):
                            dst, oth = shift[:, h, u:u + 1], neg_s[:, h, u:u + 1]
                        else:
                            dst = shift[:, bass.ds(h, 1), u:u + 1].rearrange("p a c -> p (a c)")
                            oth = neg_s[:, bass.ds(h, 1), u:u + 1].rearrange("p a c -> p (a c)")
                        dve.scalar_tensor_tensor(out=dst, in0=peak[:, par:par + 1], scalar=-SCALE, in1=oth,
                                                 op0=ALU.mult, op1=ALU.min).then_inc(S["shifted"], 1)

            dve.wait_ge(in_tab, 48)
            rotate(0, 0, True)
            rotate(1, 1, True)
            head(0, True, False)
            with dve.Fori(1, H - 1) as h:
                head(h, False, False)
            head(H - 1, False, True)
            o_evacuate(H - 1, NB - 1, H * 4 - 1)
            link(dve.tensor_tensor(e1d, shift[:, :, :].rearrange("p h t -> p (h t)"),
                                   neg_s[:, :, :].rearrange("p h t -> p (h t)"), ALU.subtract))
            dve.sem_inc(S["e1_in"], 1)
            dve.wait_ge(S["e1"], 1)
            dve.wait_ge(S["o_evac"], NB * H)
            e1v = e1.rearrange("p (h t) -> p t h", h=H)
            for n in range(NB):
                ts = slice(4 * n, 4 * n + 4)
                nm = num[:, n % 2, :]
                nm4 = nm.rearrange("p (t h d) -> p t h d", t=4, h=H)
                dn = den[:, n % 2, :].rearrange("p (t h) -> p t h", h=H)
                link(dve.tensor_tensor(dn, o_all[:, ts, :, DH], e1v[:, ts, :], ALU.add))
                link(dve.reciprocal(dn, dn))
                for i in range(4):
                    t = 4 * n + i
                    row = nm4[:, i]
                    link(dve.tensor_tensor(row, v_next[:, t, :].rearrange("p (h d) -> p h d", d=DH),
                                           e1v[:, t, :].unsqueeze(2).to_broadcast([P, H, DH]), ALU.mult))
                    link(dve.tensor_tensor(row, o_all[:, t, :, 0:DH], row, ALU.add))
                    link(dve.tensor_tensor(row, row, dn[:, i, :].unsqueeze(2).to_broadcast([P, H, DH]), ALU.mult))
                link(dve.tensor_tensor(nm, nm, ffn[:, ts, :].rearrange("p t c -> p (t c)"), ALU.mult))
                xs = x[:, ts, :].rearrange("p t c -> p (t c)")
                link(dve.scalar_tensor_tensor(out=xs, in0=nm, scalar=DEQ ** 3 / 4, in1=xs, op0=ALU.mult, op1=ALU.add))
                for t in range(4 * n, 4 * n + 4):
                    link(dve.bn_stats(stats[:, t, :], x[:, t, :]))
                    dve.bn_aggr(mean_var[:, t, :], stats[:, t, :]).then_inc(S["x2_ready"], 1)
            dve.wait_ge(S["sd2"], 1)
            link(dve.reciprocal(rstd[:, :], rstd[:, :]))
            for t in range(T):
                dve.tensor_scalar(xn[:, t, :], x[:, t, :], mean_var[:, t, 0:1], rstd[:, t:t + 1],
                                  ALU.subtract, ALU.mult).then_inc(S["xn2"], 1)
            dve.wait_ge(in_b1, 32)
            for t in range(T):
                dve.wait_ge(S["qkvd"], t + 1)
                dve.tensor_tensor(qkv[:, t, :], B(4 + t % 4)[:, 0:QKVR], b_row[:, :], ALU.add).then_inc(S["qkvb"], 1)
            dve.wait_ge(S["qkvb"], T)
            lo = qkv[:, :, 3 * D:]
            link(dve.tensor_reduce(rsum, lo, AX.X, ALU.max))
            link(dve.tensor_tensor(lg, lo, rsum.unsqueeze(2).to_broadcast([P, T, E_CNT]), ALU.subtract))
            dve.sem_inc(S["lmax"], 1)
            g4 = gt.rearrange("p t (e f) -> p t e f", e=E_CNT)
            q4 = eq.rearrange("p t (e f) -> p t e f", e=E_CNT)
            other = lo.unsqueeze(2).to_broadcast([P, T, E_CNT, E_CNT])
            own = lo.unsqueeze(3).to_broadcast([P, T, E_CNT, E_CNT])
            link(dve.tensor_tensor(g4, other, own, ALU.is_gt))
            link(dve.tensor_tensor(q4, other, own, ALU.is_equal))
            link(dve.tensor_tensor(eq, eq, tri.unsqueeze(1).to_broadcast([P, T, E_CNT * E_CNT]), ALU.mult))
            link(dve.tensor_tensor(gt, gt, eq, ALU.add))
            link(dve.tensor_reduce(rank, g4, AX.X, ALU.add))
            dve.wait_ge(S["lexp"], 1)
            link(dve.tensor_reduce(rsum, lg, AX.X, ALU.add))
            link(dve.reciprocal(rsum, rsum))
            link(dve.tensor_tensor(lg, lg, rsum.unsqueeze(2).to_broadcast([P, T, E_CNT]), ALU.mult))
            link(dve.scalar_tensor_tensor(out=gate.rearrange("p t e -> p (t e)"), in0=rank.rearrange("p t e -> p (t e)"),
                                          scalar=TOPK - 0.5, in1=lg.rearrange("p t e -> p (t e)"),
                                          op0=ALU.is_lt, op1=ALU.mult))
            for n in range(NB):
                qn = qkv[:, 4 * n:4 * n + 4, 0:D].unsqueeze(1).to_broadcast([P, NB, TPB, D])
                kn = qkv[:, :, D:2 * D].rearrange("p (m i) c -> p m i c", m=NB)
                link(dve.tensor_tensor(prod1.rearrange("p (m i c) -> p m i c", m=NB, i=TPB), qn, kn, ALU.mult))
                link(dve.tensor_reduce(sc[:, n, :, :].rearrange("p m x -> p (m x)"),
                                       prod1.rearrange("p (a d) -> p a d", d=DH), AX.X, ALU.add))
            link(dve.tensor_reduce(smax, sc.rearrange("p n m x -> p n x m"), AX.X, ALU.max))
            for n in range(NB):
                link(dve.tensor_tensor(sc[:, n], sc[:, n], smax[:, n, :].unsqueeze(1).to_broadcast([P, NB, TPB * H]), ALU.subtract))
            dve.sem_inc(S["pmax"], 1)
            dve.wait_ge(S["pexp"], 1)
            link(dve.tensor_reduce(ssum, pr.rearrange("p n m x -> p n x m"), AX.X, ALU.add))
            link(dve.reciprocal(ssum, ssum))
            for n in range(NB):
                link(dve.tensor_tensor(pr[:, n], pr[:, n], ssum[:, n, :].unsqueeze(1).to_broadcast([P, NB, TPB * H]), ALU.mult))
                vn = qkv[:, :, 2 * D:3 * D].rearrange("p t (h d) -> p t h d", d=DH)
                link(dve.tensor_tensor(prod1.rearrange("p (t h d) -> p t h d", t=T, h=H),
                                       pr[:, n].rearrange("p m (i h) -> p (m i) h", h=H).unsqueeze(3).to_broadcast([P, T, H, DH]),
                                       vn, ALU.mult))
                dve.tensor_reduce(attn[:, 4 * n:4 * n + 4, :].rearrange("p t c -> p (t c)"),
                                  prod1.rearrange("p (m x) -> p x m", m=NB), AX.X, ALU.add).then_inc(S["attn"], 1)
                dve.wait_ge(S["attn"], n + 1)
            for t in range(T):
                dve.wait_ge(S["moed"], t + 1)
                tmp = moe_tmp[:, t % 2, :]
                link(dve.tensor_tensor(tmp.rearrange("p (e c) -> p e c", e=E_CNT),
                                       bank[2 + t % 2][:, :, :].rearrange("p a (e c) -> p (a e) c", e=4),
                                       gate[:, t, :].unsqueeze(2).to_broadcast([P, E_CNT, D]), ALU.mult))
                dve.tensor_reduce(moe[:, t, :], tmp.rearrange("p (e c) -> p c e", e=E_CNT), AX.X, ALU.add)\
                    .then_inc(S["moes"], 1)
            for n in range(NB):
                ts = slice(4 * n, 4 * n + 4)
                dve.wait_ge(S["gth"], n + 1)
                dve.wait_ge(S["pj"], n + 1)
                m = moe[:, ts, :].rearrange("p t c -> p (t c)")
                at = attn[:, ts, :]
                link(dve.scalar_tensor_tensor(out=m, in0=th_moe[:, n, :], scalar=1.0, in1=m, op0=ALU.add, op1=ALU.mult))
                link(dve.tensor_tensor(at, B((2, 3, 0, 1)[n]).rearrange("p (t c) -> p t c", t=4),
                                       bp_row[:, :].unsqueeze(1).to_broadcast([P, 4, D]), ALU.add))
                at = at.rearrange("p t c -> p (t c)")
                link(dve.tensor_tensor(at, at, m, ALU.mult))
                xs = x[:, ts, :].rearrange("p t c -> p (t c)")
                dve.scalar_tensor_tensor(out=xs, in0=at, scalar=0.5, in1=xs, op0=ALU.mult, op1=ALU.add).then_inc(S["fin"], 1)

        @block.tensor
        def _(pe):
            pe.wait_ge(in_small, 16)
            for f, what, n in fills_a:
                if f >= 8:
                    after_a(pe, f - 8)
                if what == "w":
                    if n == 0:
                        pe.wait_ge(in_w0, 64)
                        pe.wait_ge(S["cast"], 3)
                    if n == 3:
                        pe.wait_ge(in_w1, 80)
                else:
                    pe.wait_ge(S["xn_ready"], 4 * n + 4)
                for j in range(4):
                    src = w_nat[:, 4 * n + j, :] if what == "w" else xn[:, 4 * n + j, :]
                    ins = pe.transpose(B(f % 8)[:, j * P:(j + 1) * P], src, ident)
                ins.then_inc(S["turned_a"], 1)
            for f in range(10):
                after_a(pe, f)
            for b in range(NB):
                for blk, bk in ((WQ, 0), (WK, 1)):
                    pe.matmul(B(2 * b + bk), wT[:, blk * D:(blk + 1) * D], xnT[:, b * L:(b + 1) * L],
                              start=True, stop=True).then_inc(S["proj"], 1)
            pe.wait_ge(S["init"], 4)
            for t in range(T):
                b8 = B(t % 8)
                if t < 8:
                    pe.wait_ge(S["part_done"], 1 + 3 * (t // 2) + (2 if t % 2 == 0 else 3))
                else:
                    pe.wait_ge(S["vt"], 2 * (t - 7))
                    pe.wait_ge(S["neg"], t - 7)
                pe.matmul(b8[:, 0:256], xnT[:, t * P:(t + 1) * P], wT[:, 0:256], start=True, stop=True)
                pe.matmul(b8[:, 256:512], xnT[:, t * P + 1:(t + 1) * P + 1], wT[:, 128:384],
                          start=True, stop=True).then_inc(S["tok"], 1)
            pe.wait_ge(S["vt"], 2 * T)
            pe.wait_ge(S["neg"], T)
            for b in range(NB):
                for k in range(3):
                    if b >= 1:
                        pe.wait_ge(S["hT"], 3 * (b - 1) + k + 1)
                    pe.matmul(B(2 * k), wT[:, (WG + k) * D:(WG + k + 1) * D], xnT[:, b * L:(b + 1) * L], start=True, stop=True)
                    pe.matmul(B(2 * k + 1), wT[:, (WU + k) * D:(WU + k + 1) * D], xnT[:, b * L:(b + 1) * L],
                              start=True, stop=True).then_inc(S["gu"], 1)
                pe.wait_ge(S["hT"], 3 * b + 3)
                if b >= 2:
                    pe.wait_ge(S["ffn_ready"], b - 1)
                for i in range(TPB):
                    for k in range(3):
                        ins = pe.matmul(B(6 + b % 2)[:, i * P:(i + 1) * P], hTt[:, k, i * P:(i + 1) * P],
                                        wT[:, (WD + k) * D:(WD + k + 1) * D], start=(k == 0), stop=(k == 2))
                ins.then_inc(S["down"], 1)

            def turn(n, par, half, first):
                if not first:
                    pe.wait_ge(S["g_rot"], n)
                cols = slice(half * 256, half * 256 + 256)
                pe.matmul(B(6)[:, 0:256], wr_st[:, 0:D], qv_st[:, par, cols], start=True, stop=True)
                pe.matmul(B(6)[:, 256:512], wr_st[:, D:2 * D], qv_st[:, par, cols], start=True, stop=True)\
                    .then_inc(S["g_done"], 1)

            def scores(U, par, spar, i, first):
                if not first:
                    pe.wait_ge(S["maxed"], U - 1)
                main, extra = bank[par][:, 0, :], bank[par][:, 1, 0:P]
                qu = qu_st[:, spar, i * P:(i + 1) * P]
                pe.matmul(main, qu, k_st[:, spar, :], start=True, stop=False)
                pe.matmul(extra, qu, k_st[:, spar, i * P:(i + 1) * P], start=True, stop=False)
                g_low, g_up = g_sb[:, spar, i * P:(i + 1) * P], g_sb[:, spar, i * P + 1:(i + 1) * P + 1]
                edge = (i + 1) * P
                pe.matmul(main[:, 0:edge], g_low, waves[:, 0, 0:edge], start=False, stop=(edge == L))
                if edge < L:
                    pe.matmul(main[:, edge:L], g_up, waves[:, 1, edge:L], start=False, stop=True)
                pe.matmul(extra, g_up, waves[:, 1, i * P:edge], start=False, stop=True)\
                    .then_inc(S["scored"], 1)

            def transpose(U, par, first):
                pe.wait_ge(S["merged"], U + 1)
                if not first:
                    pe.wait_ge(S["evaced"], U - 1)
                for c in range(TPB):
                    ins = pe.transpose(B(4 + par)[:, c * P:(c + 1) * P], prob[:, par, c * P:(c + 1) * P], ident)
                ins.then_inc(S["turned"], 1)

            def values(U, h, u, n, first):
                b, i = u // 4, u % 4
                par = u % 2
                pe.wait_ge(S["evaced"], U + 1)
                if i == 0 and not first:
                    pe.wait_ge(S["o_evac"], n)
                for c in range(TPB):
                    if isinstance(h, int):
                        v = vones[:, 4 * b + c, h, :]
                    else:
                        v = vones[:, 4 * b + c, bass.ds(h, 1), :].rearrange("p a d -> p (a d)")
                    ins = pe.matmul(B(7)[:, i * (DH + 1):(i + 1) * (DH + 1)], probT[:, par, c * P:(c + 1) * P], v,
                                    start=(c == 0), stop=(c == TPB - 1))
                ins.then_inc(S["pvd"], 1)

            def head(h, first, last):
                for b in range(NB):
                    for i in range(TPB):
                        u = 4 * b + i
                        U = h * 16 + u
                        if i in (0, 1) and not (last and b == NB - 1):
                            nb, nh = (b + 1, h) if b + 1 < NB else (0, h + 1)
                            if i == 0:
                                if nb == 0:
                                    pe.wait_ge(ld_wr, 48 * nh + 48)
                                pe.wait_ge(ldqv[nb % 2], 48 * (2 * nh + nb // 2 + 1))
                            turn(h * 8 + 2 * (b + 1) + i, nb % 2, i, False)
                        if i == 0:
                            pe.wait_ge(S["g_ready"], h * 8 + 2 * b + 2)
                            pe.wait_ge(ld[b % 2], 96 * (2 * h + b // 2 + 1))
                        scores(U, u % 2, b % 2, i, first and u < 2)
                        if not (first and u < 2):
                            transpose(U - 2, u % 2, first and u < 4)
                        if not (first and u < 3):
                            if u >= 3:
                                values(U - 3, h, u - 3, h * 4 + (u - 3) // 4, first and u < 4)
                            else:
                                values(U - 3, h - 1, 13 + u, h * 4 - 1, False)

            pe.wait_ge(S["ffn_ready"], NB)
            pe.wait_ge(in_tab, 48)
            pe.wait_ge(ld_wr, 48)
            pe.wait_ge(ldqv[0], 48)
            pe.wait_ge(S["init"], 5)
            turn(0, 0, 0, True)
            turn(1, 0, 1, False)
            head(0, True, False)
            with pe.Fori(1, H - 1) as h:
                head(h, False, False)
            head(H - 1, False, True)
            U = H * 16
            values(U - 3, H - 1, 13, H * 4 - 1, False)
            transpose(U - 2, 0, False)
            transpose(U - 1, 1, False)
            values(U - 2, H - 1, 14, H * 4 - 1, False)
            values(U - 1, H - 1, 15, H * 4 - 1, False)
            for n in range(NB):
                pe.wait_ge(S["xn2"], 4 * n + 4)
                for i in range(4):
                    ins = pe.transpose(B(n)[:, i * P:(i + 1) * P], xn[:, 4 * n + i, :], ident)
                ins.then_inc(S["turned_b"], 1)
            for t in range(T):
                if t % 4 == 0:
                    pe.wait_ge(S["evac_b"], t // 4 + 1)
                if t >= 4:
                    pe.wait_ge(S["qkvb"], t - 3)
                else:
                    pe.wait_ge(S["evaced"], H * 16)
                    pe.wait_ge(S["o_evac"], H * NB)
                pe.matmul(B(4 + t % 4)[:, 0:QKVR], xnT[:, t * P:(t + 1) * P], wT[:, WQKV * D:], start=True, stop=True)\
                    .then_inc(S["qkvd"], 1)
            pe.wait_ge(in_w1, 80)
            for n in range(2):
                for j in range(4):
                    e = 4 * n + j
                    ins = pe.matmul(B(n)[:, j * D:(j + 1) * D], wT[:, (WI + e) * D:(WI + e + 1) * D], wo1[:, e, :],
                                    start=True, stop=True)
                ins.then_inc(S["wcd"], 1)
            pe.wait_ge(S["wcb"], 2)
            for n in range(NB):
                pe.wait_ge(S["attn"], n + 1)
                if n >= 2:
                    pe.wait_ge(S["attnTs"], n - 1)
                for i in range(4):
                    ins = pe.transpose(B(n % 2)[:, i * P:(i + 1) * P], attn[:, 4 * n + i, :], ident)
                ins.then_inc(S["attnT"], 1)
            for n in range(NB):
                pe.wait_ge(S["attnTs"], NB)
                for i in range(4):
                    t = 4 * n + i
                    ins = pe.matmul(B((2, 3, 0, 1)[n])[:, i * D:(i + 1) * D], attnT[:, t * P:(t + 1) * P],
                                    wT[:, WP * D:(WP + 1) * D], start=True, stop=True)
                ins.then_inc(S["pj"], 1)
            pe.wait_ge(S["qkvb"], T)
            for t in range(T):
                if t >= 2:
                    pe.wait_ge(S["moes"], t - 1)
                for a in range(2):
                    ins = pe.matmul(bank[2 + t % 2][:, a, :], xnT[:, t * P:(t + 1) * P],
                                    wc[:, 4 * a:4 * a + 4, :].rearrange("p e c -> p (e c)"), start=True, stop=True)
                ins.then_inc(S["moed"], 1)


_INS = ["L0_attn_w", "L0_attn_Wq", "L0_attn_Wk", "L0_attn_Wv", "L0_attn_Wr", "L0_attn_u_bias", "L0_attn_v_bias",
        "L0_ffn_w_gate", "L0_ffn_w_up", "L0_ffn_w_down", "L1_attn_Wqkv", "L1_attn_bqkv", "L1_attn_Wproj",
        "L1_attn_bproj", "L1_ffn_Wr", "L1_ffn_Wi", "L1_ffn_Wo"]


def kernel(**inputs):
    import numpy as _np
    import concourse.bacc as _bacc
    from concourse import mybir as _mybir
    from concourse.bass_utils import run_bass_kernel_spmd as _run

    nc = _bacc.Bacc("TRN2", target_bir_lowering=False, num_devices=1)
    arrays, args = {}, []
    for name, a in [(n, inputs[n]) for n in _INS] + list(tables().items()):
        a = _np.ascontiguousarray(a)
        arrays[f"in_{name}"] = a
        args.append(nc.dram_tensor(f"in_{name}", a.shape, _mybir.dt.from_np(a.dtype), kind="ExternalInput").ap())
    out = nc.dram_tensor("out", (NB, L, D), _mybir.dt.float32, kind="ExternalOutput").ap()
    build(nc, *args, out)
    r = _run(nc, [arrays], core_ids=[0])
    return r.results[0]["out"]
```

```python
from contextlib import ExitStack

import numpy as np

import concourse.bass as bass
from concourse import mybir
from concourse.alu_op_type import AluOpType as ALU

ACT = mybir.ActivationFunctionType
AX = mybir.AxisListType
F32 = mybir.dt.float32
BF16 = mybir.dt.bfloat16
F16 = mybir.dt.float16
I32 = mybir.dt.int32

P = 128
NB, L, D = 4, 512, 128
H, DH = 16, 8
TPB = L // P
T = NB * TPB
HID = 384
E_CNT, TOPK = 8, 2
SCALE = 1.0 / float(np.sqrt(np.float32(DH)))
DEQ = 1.0 / 127.0
EPS = 1e-5
BIG = 1e30
G_TOP = 2.0 ** 14
P_TOP = 2.0 ** 12
SPLITS = 3
VW = SPLITS * (DH + 1)
ROWS = SPLITS * SPLITS * DH
T_LAG, LOW_LAG, V_LAG = 4, 5, 6
WIDE = L + P
WQ, WV, WK, WG, WU, WD, WI, WP, WQKV = 0, 1, 2, 3, 6, 9, 12, 20, 21
WBLOCKS = 24
QKVR = 3 * D + E_CNT


def tables():
    freq = (1.0 / 10000.0 ** (np.arange(0, D, 2, dtype=np.float64) / D)).astype(np.float32).astype(np.float64)
    f = np.repeat(freq, 2)[:, None]
    odd = (np.arange(D) % 2)[:, None]

    def waves(pos):
        return np.where(odd, np.cos(f * pos), np.sin(f * pos))

    key = np.arange(L, dtype=np.float64)[None, :]
    turn = f * (key - (L - 1))
    low = waves(key)
    up = waves(key - (2 * L - 1))
    cos_t = np.cos(turn)
    sin_t = np.where(odd, -np.sin(turn), np.sin(turn))
    rot = np.stack([np.concatenate([cos_t[:, c:c + L // 2], sin_t[:, c:c + L // 2]], 1) for c in (0, L // 2)], 1)
    mask = np.zeros((P, TPB, WIDE), np.float32)
    for tile in range(TPB):
        q = tile * P + np.arange(P)[:, None]
        k = np.arange(L)[None, :]
        bad = np.where(k < (tile + 1) * P, k > q, k < q + 2)
        mask[:, tile, :L][bad] = -BIG
        kd = tile * P + np.arange(P)[None, :]
        mask[:, tile, L:][kd < q + 2] = -BIG
    tri = np.tile((np.arange(E_CNT)[None, :] < np.arange(E_CNT)[:, None]).astype(np.float32).reshape(1, -1), (P, 1))
    last = np.zeros((P, T), np.float32)
    last[P - 1, TPB - 1::TPB] = BIG
    small = np.concatenate([np.eye(P, dtype=np.float32), tri, last], 1)

    def halves(a):
        hi = a.astype(np.float16)
        return np.stack([hi, (a - hi.astype(np.float64)).astype(np.float16)], 2)

    return {
        "c_small": small,
        "c_waves": halves(np.stack([low, up], 1)),
        "c_rot": rot.astype(np.float32),
        "c_mask": mask,
    }


def build(nc, w, Wq, Wk, Wv, Wr, u_bias, v_bias, w_gate, w_up, w_down,
          Wqkv, bqkv, Wproj, bproj, Wr1, Wi, Wo, c_small, c_waves, c_rot, c_mask, out):
    ctx = ExitStack()
    with ctx:
        def sb(name, shape, dt=F32):
            return ctx.enter_context(nc.sbuf_tensor(name, shape, dt))

        def sem(name):
            return ctx.enter_context(nc.semaphore(name))

        qv_parts = nc.dram_tensor("qv_parts", (H, NB, SPLITS, DH, L), BF16, kind="Internal").ap()
        qu_parts = nc.dram_tensor("qu_parts", (H, NB, SPLITS, DH, L), BF16, kind="Internal").ap()
        k_parts = nc.dram_tensor("k_parts", (H, NB, 5, DH, L), BF16, kind="Internal").ap()
        wr_parts = nc.dram_tensor("wr_parts", (H, 5, DH, 2 * D), BF16, kind="Internal").ap()

        x = sb("x", [P, T, D])
        eps_col = sb("eps_col", [P, 1])
        xn = sb("xn", [P, T, D])
        xnT = sb("xnT", [P, NB * L + 1])
        stats = sb("stats", [P, T, 6])
        mean_var = sb("mean_var", [P, T, 2])
        rstd = sb("rstd", [P, T])
        w_nat = sb("w_nat", [P, WBLOCKS, D])
        w_int = sb("w_int", [P, 9, D], I32)
        wT = sb("wT", [P, WBLOCKS * D + E_CNT])
        wo1 = sb("wo1", [P, E_CNT, D])
        wr_nat = sb("wr_nat", [P, 2, D])
        wr_s = sb("wr_s", [P, SPLITS, 2 * D], BF16)
        small = sb("small", [P, P + E_CNT * E_CNT + T])
        ident = small[:, 0:P]
        tri = small[:, P:P + E_CNT * E_CNT]
        last_key = small[:, P + E_CNT * E_CNT:]
        waves = sb("waves", [P, 2, 2, L], F16)
        rot = sb("rot", [P, 2, L])
        mask = sb("mask", [P, TPB, WIDE])
        ub_col = sb("ub_col", [P, 1])
        vb_col = sb("vb_col", [P, 1])
        ub_row = sb("ub_row", [P, D])
        b_row = sb("b_row", [P, QKVR])
        bp_row = sb("bp_row", [P, D])
        arena = sb("arena", [P, 3 * NB * SPLITS * L // 2])
        parts = arena[:, :].bitcast(BF16).rearrange("p (a b s n) -> p a b s n", a=3, b=NB, s=SPLITS)
        qkv = arena[:, 0:T * QKVR].rearrange("p (t c) -> p t c", t=T)
        rest = sb("rest", [P, 2, L])
        v_parts = sb("v_parts", [P, T, H, VW], BF16)
        v_now = sb("v_now", [P, 2, D])
        norms = sb("norms", [P, 2])
        reach = sb("reach", [P, 1])
        sigma = sb("sigma", [P, 1])
        scale_in = sb("scale_in", [P, 1])
        scale_neg = sb("scale_neg", [P, 1])
        ones = sb("ones", [P, P])
        v_next = sb("v_next", [P, T, D])
        neg_s = sb("neg_s", [P, H, T])
        shift = sb("shift", [P, H, T])
        ffn = sb("ffn", [P, T, D])
        o_all = sb("o_all", [P, T, H, DH + 1])
        qu_st = sb("qu_st", [ROWS, 2, L], BF16)
        qv_st = sb("qv_st", [ROWS, 2, L], BF16)
        k_st = sb("k_st", [ROWS, 2, L], BF16)
        wr_st = sb("wr_st", [ROWS, H, 2 * D], BF16)
        work = sb("work", [P, 7680])

        def area(at, *shape):
            n = int(np.prod(shape))
            names = "abcd"[:len(shape)]
            return work[:, at:at + n].rearrange(f"p ({' '.join(names)}) -> p {' '.join(names)}",
                                                **dict(zip(names, shape)))

        turned_g = area(0, 2, L)
        g_sum = area(1024, 2, L // 2)
        s_sb = area(1536, 4, WIDE)
        prob = arena[:, 6656:6656 + 4 * WIDE].rearrange("p (a n) -> p a n", a=4)
        probT = area(4096, 4, L).bitcast(F16).rearrange("p a (s n) -> p a s n", s=2)
        g_sb = area(6144, 2, 2 * L // 2 + 2).bitcast(F16).rearrange("p a (s n) -> p a s n", s=2)
        peak = sb("peak", [P, 2])
        pace = sb("pace", [P, 2])

        bank = [ctx.enter_context(nc.psum_tensor(f"bank{i}", [P, 2, 512], F32)) for i in range(4)]

        def B(i):
            return bank[i // 2][:, i % 2, :]

        in_x = [sem(f"in_x{i}") for i in range(2)]
        in_w0, in_wint, in_w1, in_small, in_tab, in_bias, in_b1 = (
            sem(n) for n in ("in_w0", "in_wint", "in_w1", "in_small", "in_tab", "in_bias", "in_b1"))
        block = ctx.enter_context(nc.Block())

        S = {}

        def s_(name):
            if name not in S:
                S[name] = sem(name)
            return S[name]

        names = ["cast", "g_sum", "norm_in", "norm", "reach_in", "reach", "sigma", "v_split", "hi_done", "dve_self", "sd", "xn_ready", "turned_a", "evac_v", "evac_a", "proj", "part1", "part_done",
                 "scr", "wr_done", "init", "tok", "vt", "qk", "neg", "gu", "th", "hT", "down", "th2", "ffn_ready",
                 "g_done", "g_rot", "g_ready", "scored", "maxed", "shifted", "exped", "merged", "turned", "evaced",
                 "pvd", "o_evac", "e1_in", "e1", "x2_ready", "sd2", "xn2", "turned_b", "evac_b", "qkvd", "qkvb",
                 "wcd", "wcb", "moed", "moes", "lmax", "lexp", "pmax", "pexp", "attn", "attnT", "attnTs", "pj",
                 "res", "gth", "fin", "stored"]
        for n in names:
            s_(n)
        ld = [sem(f"ld{i}") for i in range(2)]
        ldqv = [sem(f"ldqv{i}") for i in range(2)]
        ld_wr = sem("ld_wr")

        xr = w.rearrange("b (i p) c -> p (b i) c", p=P)
        outr = out.rearrange("b (i p) c -> p (b i) c", p=P)
        fills_a = [(0, "w", 0)] + [(i, "x", i - 1) for i in range(1, 5)] + [(i, "w", i - 4) for i in range(5, 10)]
        dve_fills = [f for f, _, _ in fills_a if f % 2 == 1]
        act_fills = [f for f, _, _ in fills_a if f % 2 == 0]

        def after_a(eng, f):
            if f % 2:
                eng.wait_ge(S["evac_v"], dve_fills.index(f) + 1)
            else:
                eng.wait_ge(S["evac_a"], act_fills.index(f) + 1)

        prod0 = area(0, T, D)
        tq = area(2048, 2, D)
        s_next = work[:, 2304:2560]
        th = area(2560, 3, L)
        hg = area(4096, 2, L)
        hTt = area(5120, 3, L)
        th2 = area(6656, 2, L)
        e1d = work[:, 0:H * T]
        e1 = work[:, 256:256 + H * T]
        num = area(512, 2, L)
        den = area(1536, 2, TPB * H)
        prod1 = area(2048, 2048)
        sc = area(4096, NB, NB, TPB * H)
        pr = area(5120, NB, NB, TPB * H)
        smax = area(6144, NB, TPB * H)
        ssum = area(6400, NB, TPB * H)
        gate = area(6656, T, E_CNT)
        rank = area(6784, T, E_CNT)
        rsum = area(6912, T)
        lg = area(6928, T, E_CNT)
        gt = area(2048, T, E_CNT * E_CNT)
        eq = area(3072, T, E_CNT * E_CNT)
        moe_tmp = area(2048, 2, E_CNT * D)
        attn = v_next
        attnT = ffn[:, :, :].rearrange("p t c -> p (t c)")
        moe = xn
        th_moe = o_all[:, :, :, :].rearrange("p t h d -> p (t h d)")[:, 0:T * D].rearrange("p (n c) -> p n c", n=NB)
        wc = w_nat[:, 0:E_CNT, :]

        @block.sync
        def _(sp):
            sp.dma_start(x[:, 0:8, :], xr[:, 0:8, :]).then_inc(in_x[0], 16)
            sp.dma_start(w_nat[:, WQ, :], Wq).then_inc(in_w0, 16)
            sp.dma_start(w_nat[:, WV, :], Wv).then_inc(in_w0, 16)
            sp.dma_start(w_nat[:, WK, :], Wk).then_inc(in_w0, 16)
            sp.dma_start(wr_nat[:, 0, :], Wr).then_inc(in_w0, 16)
            sp.dma_start(x[:, 8:16, :], xr[:, 8:16, :]).then_inc(in_x[1], 16)
            sp.dma_start(waves[:, :, :], c_waves).then_inc(in_tab, 16)
            sp.dma_start(rot[:, :, :], c_rot).then_inc(in_tab, 16)
            sp.dma_start(mask[:, :, :], c_mask).then_inc(in_tab, 16)
            sp.dma_start(w_nat[:, WI:WI + E_CNT, :], Wi.rearrange("e d h -> d e h")).then_inc(in_w1, 16)
            sp.dma_start(w_nat[:, WP, :], Wproj).then_inc(in_w1, 16)
            sp.dma_start(w_nat[:, WQKV:WQKV + 3, :], Wqkv.rearrange("(k p) c -> p k c", p=P)).then_inc(in_w1, 16)
            sp.dma_start(wT[:, WBLOCKS * D:], Wr1).then_inc(in_w1, 16)
            sp.dma_start(wo1[:, :, :], Wo.rearrange("e h d -> h e d")).then_inc(in_w1, 16)

            def piece(scr, h, b, lo, hi):
                at = scr[h:h + 1, b] if isinstance(h, int) else scr[bass.ds(h, 1), b]
                return at[:, lo:hi].rearrange("a s d n -> (a s d) n")

            def load_qv(h, b, base):
                if base is not None:
                    sp.wait_ge(S["g_done"], base)
                for r in range(SPLITS):
                    rows = slice(r * SPLITS * DH, (r + 1) * SPLITS * DH)
                    sp.dma_start(qv_st[rows, b % 2, :], piece(qv_parts, h, b, 0, 3)).then_inc(ldqv[b % 2], 16)

            def load_quk(h, b, base):
                if base is not None:
                    sp.wait_ge(S["scored"], base)
                for r in range(SPLITS):
                    rows = slice(r * SPLITS * DH, (r + 1) * SPLITS * DH)
                    sp.dma_start(qu_st[rows, b % 2, :], piece(qu_parts, h, b, 0, 3)).then_inc(ld[b % 2], 16)
                    sp.dma_start(k_st[rows, b % 2, :], piece(k_parts, h, b, r, r + 3)).then_inc(ld[b % 2], 16)

            sp.wait_ge(S["wr_done"], 16 * 5)
            for r in range(SPLITS):
                rows = slice(r * SPLITS * DH, (r + 1) * SPLITS * DH)
                sp.dma_start(wr_st[rows, :, :], wr_parts[:, r:r + 3].rearrange("h s d n -> (s d) h n")).then_inc(ld_wr, 16)
            sp.wait_ge(S["scr"], 16 * NB * 11)
            for b in range(NB):
                load_qv(0, b, 2 * (b - 1) if b >= 2 else None)
                if b >= 1:
                    load_quk(0, b - 1, 4 * (b - 2) if b >= 3 else None)
            with sp.Fori(1, H) as h:
                for b in range(NB):
                    load_qv(h, b, h * 8 + 2 * (b - 1))
                    if b == 0:
                        load_quk(h - 1, NB - 1, h * 16 - 8)
                    else:
                        load_quk(h, b - 1, h * 16 + 4 * (b - 2))
            load_quk(H - 1, NB - 1, H * 16 - 8)
            sp.wait_ge(S["fin"], NB)
            sp.dma_start(outr, x[:, :, :]).then_inc(S["stored"], 16)
            sp.wait_ge(S["stored"], 16)

        @block.gpsimd
        def _(pool):
            pool.memset(eps_col[:, :], EPS).then_inc(S["init"], 1)
            pool.memset(b_row[:, 3 * D:], 0.0).then_inc(S["init"], 1)
            pool.memset(xnT[:, NB * L:], 0.0).then_inc(S["init"], 1)
            pool.memset(ones[:, :], 1.0).then_inc(S["init"], 1)
            pool.memset(v_parts[:, :, :, DH:DH + 1], 1.0).then_inc(S["init"], 1)
            pool.memset(v_parts[:, :, :, 2 * DH + 1:2 * DH + 2], 0.0).then_inc(S["init"], 1)
            pool.memset(v_parts[:, :, :, 3 * DH + 2:], 0.0).then_inc(S["init"], 1)
            pool.dma_start(small[:, :], c_small).then_inc(in_small, 16)
            pool.dma_start(w_int[:, 0:3, :], w_gate.rearrange("(k p) c -> p k c", p=P)).then_inc(in_wint, 16)
            pool.dma_start(w_int[:, 3:6, :], w_up.rearrange("(k p) c -> p k c", p=P)).then_inc(in_wint, 16)
            pool.dma_start(w_int[:, 6:9, :], w_down.rearrange("d (k h) -> d k h", k=3)).then_inc(in_wint, 16)
            pool.dma_start(ub_col[:, :], u_bias.rearrange("h (d o) -> (h d) o", o=1)).then_inc(in_bias, 16)
            pool.dma_start(vb_col[:, :], v_bias.rearrange("h (d o) -> (h d) o", o=1)).then_inc(in_bias, 16)
            pool.dma_start(ub_row[:, :], u_bias.rearrange("h d -> (h d)").partition_broadcast(P)).then_inc(in_bias, 16)
            pool.dma_start(b_row[:, 0:3 * D], bqkv.partition_broadcast(P)).then_inc(in_b1, 16)
            pool.dma_start(bp_row[:, :], bproj.partition_broadcast(P)).then_inc(in_b1, 16)
            pool.wait_ge(S["part_done"], 1)
            for s in range(5):
                pool.dma_start(wr_parts[:, s], wr_s[:, s % 3, :]).then_inc(S["wr_done"], 16)
            for b in range(NB):
                for kind, (scr, n) in enumerate(((qv_parts, 3), (qu_parts, 3), (k_parts, 5))):
                    pool.wait_ge(S["part_done"], 2 + 3 * b + kind)
                    for s in range(n):
                        pool.dma_start(scr[:, b, s], parts[:, kind, b, s % 3, :]).then_inc(S["scr"], 16)

            def rotate(n, par, half, free):
                pool.wait_ge(S["g_rot"], n + 1)
                if free is not None:
                    pool.wait_ge(S["scored"], free)
                cols = slice(half * 256, half * 256 + 256)
                pool.tensor_tensor(g_sum[:, half, :], turned_g[:, half, 0:256], turned_g[:, half, 256:512],
                                   ALU.add).then_inc(S["g_sum"], 1)
                pool.tensor_tensor(g_sb[:, par, 0, cols], turned_g[:, half, 0:256], turned_g[:, half, 256:512],
                                   ALU.add).then_inc(S["g_sum"], 1)
                pool.wait_ge(S["g_sum"], 2 * n + 2)
                pool.tensor_tensor(g_sb[:, par, 1, cols], g_sum[:, half, :], g_sb[:, par, 0, cols],
                                   ALU.subtract).then_inc(S["g_ready"], 1)

            def merge(U, i):
                pool.wait_ge(S["exped"], U + 1)
                cols = slice(i * P, i * P + P)
                pool.tensor_tensor(prob[:, i, cols], prob[:, i, cols], prob[:, i, L:WIDE],
                                   ALU.add).then_inc(S["merged"], 1)

            def head(h, first, last):
                for b in range(NB):
                    for i in range(TPB):
                        ahead = {1: 1, 3: 2}.get(i)
                        if ahead and not (last and b + ahead >= NB):
                            free = None if first and b + ahead < 2 else h * 16 + 4 * (b + ahead - 1)
                            rotate(h * 8 + 2 * (b + ahead) + (i == 1), (b + ahead) % 2, int(i == 1), free)
                        merge(h * 16 + 4 * b + i, i)

            pool.wait_ge(S["ffn_ready"], NB)
            pool.memset(g_sb[:, :, :, L:], 0.0).then_inc(S["init"], 1)
            rotate(0, 0, 0, None)
            rotate(1, 0, 1, None)
            rotate(2, 1, 0, None)
            head(0, True, False)
            with pool.Fori(1, H - 1) as h:
                head(h, False, False)
            head(H - 1, False, True)

        @block.scalar
        def _(act):
            act.wait_ge(S["init"], 7)
            act.wait_ge(S["norm_in"], 2)
            act.activation(norms[:, :], norms[:, :], ACT.Sqrt).then_inc(S["norm"], 1)
            act.wait_ge(S["dve_self"], 2 * T)
            act.activation(rstd[:, :], mean_var[:, :, 1], ACT.Sqrt, bias=eps_col[:, 0:1]).then_inc(S["sd"], 1)
            for f, what, n in fills_a:
                if f % 2 == 0:
                    act.wait_ge(S["turned_a"], f + 1)
                    dst = wT[:, n * 512:(n + 1) * 512] if what == "w" else xnT[:, n * 512:(n + 1) * 512]
                    act.activation(dst, B(f % 8), ACT.Copy).then_inc(S["evac_a"], 1)
            act.wait_ge(in_w0, 64)
            act.wait_ge(S["cast"], 5)
            act.activation(wr_s[:, 0, :], wr_nat[:, :, :], ACT.Copy).then_inc(S["part1"], 1)
            act.wait_ge(S["sigma"], 1)
            for b in range(NB):
                for kind in range(3):
                    act.wait_ge(S["proj"], 2 * b + (1 if kind < 2 else 2))
                    src = B(2 * b + (kind == 2))
                    if kind < 2:
                        act.activation(parts[:, kind, b, 0, :], src, ACT.Identity,
                                       bias=(vb_col, ub_col)[kind][:, 0:1]).then_inc(S["part1"], 1)
                    else:
                        act.activation(parts[:, kind, b, 0, :], src, ACT.Copy).then_inc(S["part1"], 1)
            for t in range(T):
                act.wait_ge(S["tok"], t + 1)
                if t >= 2:
                    act.wait_ge(S["v_split"], t - 1)
                act.activation(v_now[:, t % 2, :], B(t % 8)[:, 128:256], ACT.Copy).then_inc(S["vt"], 1)
                act.activation(v_next[:, t, :], B(t % 8)[:, 256:384], ACT.Copy).then_inc(S["vt"], 1)
            for b in range(NB):
                for k in range(3):
                    j = 3 * b + k
                    act.wait_ge(S["gu"], j + 1)
                    if j >= 3:
                        act.wait_ge(S["hT"], j - 2)
                    act.activation(th[:, j % 3, :], B(2 * k), ACT.Tanh, scale=DEQ / 2).then_inc(S["th"], 1)
                act.wait_ge(S["down"], b + 1)
                if b >= 2:
                    act.wait_ge(S["ffn_ready"], b - 1)
                act.activation(th2[:, b % 2, :], B(6 + b % 2), ACT.Tanh, scale=DEQ ** 3 / 4).then_inc(S["th2"], 1)

            def high_half(U, u, first):
                act.wait_ge(S["turned"], U + 1)
                if not first:
                    act.wait_ge(S["pvd"], U - 3)
                act.activation(probT[:, u % 4, 0, :], B(4 + u % 2), ACT.Copy, scale=P_TOP).then_inc(S["hi_done"], 1)

            def head(h, first):
                for b in range(NB):
                    for i in range(TPB):
                        u = 4 * b + i
                        U = h * 16 + u
                        if not (first and u < T_LAG):
                            high_half(U - T_LAG, (u - T_LAG) % 4, first and u < T_LAG + 4)
                        act.wait_ge(S["shifted"], U + 1)
                        if not (first and u < 4):
                            act.wait_ge(S["turned"], U - 3)
                        bias = shift[:, h, u:u + 1] if isinstance(h, int) else shift[:, bass.ds(h, 1), u:u + 1]
                        act.activation(prob[:, i, :], s_sb[:, i, :], ACT.Exp, bias=bias,
                                       scale=scale_in[:, 0:1]).then_inc(S["exped"], 1)

            head(0, True)
            with act.Fori(1, H) as h:
                head(h, False)
            for back in range(T_LAG, 0, -1):
                high_half(H * 16 - back, -back % 4, False)
            act.wait_ge(S["e1_in"], 1)
            act.activation(e1, e1d, ACT.Exp).then_inc(S["e1"], 1)
            act.wait_ge(S["x2_ready"], T)
            act.activation(rstd[:, :], mean_var[:, :, 1], ACT.Sqrt, bias=eps_col[:, 0:1]).then_inc(S["sd2"], 1)
            for n in range(NB):
                act.wait_ge(S["turned_b"], n + 1)
                act.activation(xnT[:, n * L:(n + 1) * L], B(n), ACT.Copy).then_inc(S["evac_b"], 1)
            for n in range(2):
                act.wait_ge(S["wcd"], n + 1)
                act.activation(wc[:, 4 * n:4 * n + 4, :].rearrange("p e c -> p (e c)"), B(n), ACT.Copy).then_inc(S["wcb"], 1)
            act.wait_ge(S["lmax"], 1)
            act.activation(lg, lg, ACT.Exp).then_inc(S["lexp"], 1)
            act.wait_ge(S["pmax"], 1)
            act.activation(pr, sc, ACT.Exp, scale=SCALE).then_inc(S["pexp"], 1)
            for n in range(NB):
                act.wait_ge(S["attnT"], n + 1)
                act.activation(attnT[:, n * L:(n + 1) * L], B(n % 2), ACT.Copy).then_inc(S["attnTs"], 1)
            for n in range(NB):
                act.wait_ge(S["moes"], 4 * n + 4)
                act.activation(th_moe[:, n, :], moe[:, 4 * n:4 * n + 4, :].rearrange("p t c -> p (t c)"), ACT.Tanh,
                               scale=0.5).then_inc(S["gth"], 1)

        @block.vector
        def _(dve):
            c = [0]

            def link(ins):
                c[0] += 1
                ins.then_inc(S["qk"], 1)
                dve.wait_ge(S["qk"], c[0])

            dve.wait_ge(in_w0, 64)
            for k, src in enumerate((w_nat[:, WQ, :], wr_nat[:, 0, :])):
                dve.tensor_tensor_reduce(rest[:, k, 0:D], src, src, 1.0, 0.0, ALU.mult, ALU.add, norms[:, k:k + 1])\
                    .then_inc(S["norm_in"], 1)
            for half in range(2):
                dve.wait_ge(in_x[half], 16)
                for t in range(8 * half, 8 * half + 8):
                    dve.bn_stats(stats[:, t, :], x[:, t, :]).then_inc(S["dve_self"], 1)
            for t in range(T):
                dve.wait_ge(S["dve_self"], T)
                dve.bn_aggr(mean_var[:, t, :], stats[:, t, :]).then_inc(S["dve_self"], 1)
            dve.wait_ge(in_bias, 48)
            dve.wait_ge(S["norm"], 1)
            link(dve.scalar_tensor_tensor(out=reach[:, :], in0=vb_col[:, :], scalar=-1.0, in1=vb_col[:, :],
                                          op0=ALU.mult, op1=ALU.max))
            link(dve.scalar_tensor_tensor(out=reach[:, :], in0=norms[:, 0:1], scalar=float(np.sqrt(D)), in1=reach[:, :],
                                          op0=ALU.mult, op1=ALU.add))
            dve.tensor_tensor(reach[:, :], reach[:, :], norms[:, 1:2], ALU.mult).then_inc(S["reach_in"], 1)
            dve.wait_ge(S["reach"], 1)
            link(dve.tensor_scalar(sigma[:, :], B(7)[:, 0:1], 4.0, 1.0 / G_TOP, ALU.max, ALU.mult))
            link(dve.tensor_scalar(scale_in[:, :], sigma[:, :], SCALE, None, ALU.mult))
            link(dve.tensor_scalar(scale_neg[:, :], sigma[:, :], -SCALE, None, ALU.mult))
            link(dve.reciprocal(sigma[:, :], sigma[:, :]))
            link(dve.tensor_scalar(ub_row[:, :], ub_row[:, :], sigma[:, 0:1], None, ALU.mult))
            link(dve.tensor_tensor(ub_col[:, :], ub_col[:, :], sigma[:, :], ALU.mult))
            link(dve.tensor_tensor(vb_col[:, :], vb_col[:, :], sigma[:, :], ALU.mult))
            dve.wait_ge(in_wint, 48)
            for k in range(3):
                dve.tensor_copy(w_nat[:, WG + 3 * k:WG + 3 * k + 3, :], w_int[:, 3 * k:3 * k + 3, :]).then_inc(S["cast"], 1)
            dve.wait_ge(in_w0, 64)
            pair = wr_nat[:, 0, :].rearrange("p (k two) -> p k two", two=2)
            swap = wr_nat[:, 1, :].rearrange("p (k two) -> p k two", two=2)
            dve.tensor_copy(swap[:, :, 0], pair[:, :, 1]).then_inc(S["cast"], 1)
            dve.tensor_copy(swap[:, :, 1], pair[:, :, 0]).then_inc(S["cast"], 1)
            dve.wait_ge(S["sd"], 1)
            dve.reciprocal(rstd[:, :], rstd[:, :]).then_inc(S["dve_self"], 1)
            dve.wait_ge(S["dve_self"], 2 * T + 1)
            for t in range(T):
                dve.tensor_scalar(xn[:, t, :], x[:, t, :], mean_var[:, t, 0:1], rstd[:, t:t + 1],
                                  ALU.subtract, ALU.mult).then_inc(S["xn_ready"], 1)
            for f, what, n in fills_a:
                if f % 2 == 1:
                    dve.wait_ge(S["turned_a"], f + 1)
                    dst = wT[:, n * 512:(n + 1) * 512] if what == "w" else xnT[:, n * 512:(n + 1) * 512]
                    dve.tensor_copy(dst, B(f % 8)).then_inc(S["evac_v"], 1)
            dve.wait_ge(S["evac_a"], 1)
            link(dve.tensor_scalar(wT[:, WQ * D:(WQ + 1) * D], wT[:, WQ * D:(WQ + 1) * D], sigma[:, 0:1], None, ALU.mult))
            dve.sem_inc(S["sigma"], 1)
            dve.wait_ge(S["part1"], 1)
            r = rest[:, 0, 0:2 * D]
            link(dve.tensor_tensor(r, wr_nat[:, :, :].rearrange("p a c -> p (a c)"), wr_s[:, 0, :], ALU.subtract))
            link(dve.tensor_copy(wr_s[:, 1, :], r))
            dve.tensor_tensor(wr_s[:, 2, :], r, wr_s[:, 1, :], ALU.subtract).then_inc(S["part_done"], 1)
            dve.wait_ge(in_bias, 48)
            for b in range(NB):
                for kind in range(3):
                    n = 1 + 3 * b + kind
                    dve.wait_ge(S["part1"], n + 2 if kind == 0 else n + 1)
                    r = rest[:, n % 2, :]
                    src = B(2 * b + (kind == 2))
                    s1, s2, s3 = (parts[:, kind, b, s, :] for s in range(3))
                    if n >= 2:
                        dve.wait_ge(S["part_done"], n - 1)
                    if kind < 2:
                        link(dve.scalar_tensor_tensor(out=r, in0=src, scalar=(vb_col, ub_col)[kind][:, 0:1], in1=s1,
                                                      op0=ALU.add, op1=ALU.subtract))
                    else:
                        link(dve.tensor_tensor(r, src, s1, ALU.subtract))
                    link(dve.tensor_copy(s2, r))
                    dve.tensor_tensor(s3, r, s2, ALU.subtract).then_inc(S["part_done"], 1)
            for t in range(T):
                dve.wait_ge(S["vt"], 2 * t + 2)
                link(dve.tensor_tensor(tq[:, t % 2, :], B(t % 8)[:, 0:128], ub_row[:, :], ALU.add))
                dve.tensor_tensor(prod0[:, t, :], B(t % 8)[:, 384:512], tq[:, t % 2, :], ALU.mult).then_inc(S["neg"], 1)
                vn = v_now[:, t % 2, :].rearrange("p (h d) -> p h d", h=H)
                v1, v2, v3 = (v_parts[:, t, :, (DH + 1) * k:(DH + 1) * k + DH] for k in range(3))
                link(dve.tensor_copy(v1, vn))
                link(dve.tensor_tensor(vn, vn, v1, ALU.subtract))
                link(dve.tensor_copy(v2, vn))
                dve.tensor_tensor(v3, vn, v2, ALU.subtract).then_inc(S["v_split"], 1)
            dve.wait_ge(S["neg"], T)
            link(dve.tensor_reduce(s_next, prod0.rearrange("p t (h d) -> p (t h) d", d=DH), AX.X, ALU.add))
            dve.wait_ge(in_small, 16)
            link(dve.tensor_scalar(s_next, s_next, scale_neg[:, 0:1], None, ALU.mult))
            link(dve.tensor_tensor(neg_s[:, :, :].rearrange("p h t -> p t h"),
                                   s_next.rearrange("p (t h) -> p t h", h=H),
                                   last_key.unsqueeze(2).to_broadcast([P, T, H]), ALU.add))
            for b in range(NB):
                for k in range(3):
                    j = 3 * b + k
                    dve.wait_ge(S["th"], j + 1)
                    link(dve.scalar_tensor_tensor(out=hg[:, j % 2, :], in0=th[:, j % 3, :], scalar=1.0, in1=B(2 * k),
                                                  op0=ALU.add, op1=ALU.mult))
                    if b >= 1:
                        dve.wait_ge(S["down"], b)
                    dve.tensor_tensor(hTt[:, k, :], B(2 * k + 1), hg[:, j % 2, :], ALU.mult).then_inc(S["hT"], 1)
                dve.wait_ge(S["th2"], b + 1)
                dve.scalar_tensor_tensor(out=ffn[:, 4 * b:4 * b + 4, :].rearrange("p t c -> p (t c)"), in0=th2[:, b % 2, :],
                                         scalar=1.0, in1=B(6 + b % 2), op0=ALU.add, op1=ALU.mult).then_inc(S["ffn_ready"], 1)

            def rotate(n, half, first):
                dve.wait_ge(S["g_done"], n + 1)
                if not first:
                    dve.wait_ge(S["g_ready"], n - 1)
                dve.tensor_tensor(turned_g[:, half, :], B(6), rot[:, half, :], ALU.mult).then_inc(S["g_rot"], 1)

            def o_evacuate(h, b, n):
                dve.wait_ge(S["pvd"], 4 * n + 4)
                dst = o_all[:, 4 * b:4 * b + 4, h, :] if isinstance(h, int) else o_all[:, 4 * b:4 * b + 4, bass.ds(h, 1), :]
                src = B(7)[:, 0:4 * VW].rearrange("p (i s d) -> p i d s", i=4, s=SPLITS)
                if not isinstance(h, int):
                    dst = dst.rearrange("p i a d -> p i (a d)")
                dve.tensor_reduce(dst, src, AX.X, ALU.add).then_inc(S["o_evac"], 1)

            def low_half(U, u):
                dve.wait_ge(S["hi_done"], U + 1)
                dve.scalar_tensor_tensor(out=probT[:, u % 4, 1, :], in0=B(4 + u % 2), scalar=P_TOP, in1=probT[:, u % 4, 0, :],
                                         op0=ALU.mult, op1=ALU.subtract).then_inc(S["evaced"], 1)

            def head(h, first, last):
                for b in range(NB):
                    for i in range(TPB):
                        u = 4 * b + i
                        U = h * 16 + u
                        par = u % 2
                        if i in (0, 2) and not (last and b == NB - 1):
                            rotate(h * 8 + 2 * (b + 1) + i // 2, i // 2, False)
                        if i == V_LAG % TPB and not (first and b < 2):
                            if b >= 2:
                                o_evacuate(h, b - 2, h * 4 + b - 2)
                            else:
                                o_evacuate(h - 1, b + 2, h * 4 + b - 2)
                        dve.wait_ge(S["scored"], U + 1)
                        if not (first and u < 4):
                            dve.wait_ge(S["exped"], U - 3)
                        dve.memset(pace[:, par:par + 1], 0.0)
                        dve.tensor_tensor_reduce(s_sb[:, i, :], bank[par][:, :, :].rearrange("p a c -> p (a c)")[:, 0:WIDE],
                                                 mask[:, i, :], 1.0, -3e38, ALU.add, ALU.max,
                                                 peak[:, par:par + 1]).then_inc(S["maxed"], 1)
                        if not (first and u < LOW_LAG):
                            low_half(U - LOW_LAG, (u - LOW_LAG) % 4)
                        dve.wait_ge(S["maxed"], U + 1)
                        if isinstance(h, int):
                            dst, oth = shift[:, h, u:u + 1], neg_s[:, h, u:u + 1]
                        else:
                            dst = shift[:, bass.ds(h, 1), u:u + 1].rearrange("p a c -> p (a c)")
                            oth = neg_s[:, bass.ds(h, 1), u:u + 1].rearrange("p a c -> p (a c)")
                        dve.scalar_tensor_tensor(out=dst, in0=peak[:, par:par + 1], scalar=scale_neg[:, 0:1], in1=oth,
                                                 op0=ALU.mult, op1=ALU.min).then_inc(S["shifted"], 1)

            dve.wait_ge(in_tab, 48)
            rotate(0, 0, True)
            rotate(1, 1, True)
            head(0, True, False)
            with dve.Fori(1, H - 1) as h:
                head(h, False, False)
            head(H - 1, False, True)
            for back in range(LOW_LAG, 0, -1):
                if back == TPB - 1:
                    o_evacuate(H - 1, NB - 2, H * 4 - 2)
                low_half(H * 16 - back, -back % 4)
            o_evacuate(H - 1, NB - 1, H * 4 - 1)
            link(dve.tensor_tensor(e1d, shift[:, :, :].rearrange("p h t -> p (h t)"),
                                   neg_s[:, :, :].rearrange("p h t -> p (h t)"), ALU.subtract))
            dve.sem_inc(S["e1_in"], 1)
            dve.wait_ge(S["e1"], 1)
            dve.wait_ge(S["o_evac"], NB * H)
            link(dve.tensor_scalar(e1, e1, P_TOP, None, ALU.mult))
            e1v = e1.rearrange("p (h t) -> p t h", h=H)
            for n in range(NB):
                ts = slice(4 * n, 4 * n + 4)
                nm = num[:, n % 2, :]
                nm4 = nm.rearrange("p (t h d) -> p t h d", t=4, h=H)
                dn = den[:, n % 2, :].rearrange("p (t h) -> p t h", h=H)
                link(dve.tensor_tensor(dn, o_all[:, ts, :, DH], e1v[:, ts, :], ALU.add))
                link(dve.reciprocal(dn, dn))
                for i in range(4):
                    t = 4 * n + i
                    row = nm4[:, i]
                    link(dve.tensor_tensor(row, v_next[:, t, :].rearrange("p (h d) -> p h d", d=DH),
                                           e1v[:, t, :].unsqueeze(2).to_broadcast([P, H, DH]), ALU.mult))
                    link(dve.tensor_tensor(row, o_all[:, t, :, 0:DH], row, ALU.add))
                    link(dve.tensor_tensor(row, row, dn[:, i, :].unsqueeze(2).to_broadcast([P, H, DH]), ALU.mult))
                link(dve.tensor_tensor(nm, nm, ffn[:, ts, :].rearrange("p t c -> p (t c)"), ALU.mult))
                xs = x[:, ts, :].rearrange("p t c -> p (t c)")
                link(dve.scalar_tensor_tensor(out=xs, in0=nm, scalar=DEQ ** 3 / 4, in1=xs, op0=ALU.mult, op1=ALU.add))
                for t in range(4 * n, 4 * n + 4):
                    link(dve.bn_stats(stats[:, t, :], x[:, t, :]))
                    dve.bn_aggr(mean_var[:, t, :], stats[:, t, :]).then_inc(S["x2_ready"], 1)
            dve.wait_ge(S["sd2"], 1)
            link(dve.reciprocal(rstd[:, :], rstd[:, :]))
            for t in range(T):
                dve.tensor_scalar(xn[:, t, :], x[:, t, :], mean_var[:, t, 0:1], rstd[:, t:t + 1],
                                  ALU.subtract, ALU.mult).then_inc(S["xn2"], 1)
            dve.wait_ge(in_b1, 32)
            for t in range(T):
                dve.wait_ge(S["qkvd"], t + 1)
                dve.tensor_tensor(qkv[:, t, :], B(4 + t % 4)[:, 0:QKVR], b_row[:, :], ALU.add).then_inc(S["qkvb"], 1)
            dve.wait_ge(S["qkvb"], T)
            lo = qkv[:, :, 3 * D:]
            link(dve.tensor_reduce(rsum, lo, AX.X, ALU.max))
            link(dve.tensor_tensor(lg, lo, rsum.unsqueeze(2).to_broadcast([P, T, E_CNT]), ALU.subtract))
            dve.sem_inc(S["lmax"], 1)
            g4 = gt.rearrange("p t (e f) -> p t e f", e=E_CNT)
            q4 = eq.rearrange("p t (e f) -> p t e f", e=E_CNT)
            other = lo.unsqueeze(2).to_broadcast([P, T, E_CNT, E_CNT])
            own = lo.unsqueeze(3).to_broadcast([P, T, E_CNT, E_CNT])
            link(dve.tensor_tensor(g4, other, own, ALU.is_gt))
            link(dve.tensor_tensor(q4, other, own, ALU.is_equal))
            link(dve.tensor_tensor(eq, eq, tri.unsqueeze(1).to_broadcast([P, T, E_CNT * E_CNT]), ALU.mult))
            link(dve.tensor_tensor(gt, gt, eq, ALU.add))
            link(dve.tensor_reduce(rank, g4, AX.X, ALU.add))
            dve.wait_ge(S["lexp"], 1)
            link(dve.tensor_reduce(rsum, lg, AX.X, ALU.add))
            link(dve.reciprocal(rsum, rsum))
            link(dve.tensor_tensor(lg, lg, rsum.unsqueeze(2).to_broadcast([P, T, E_CNT]), ALU.mult))
            link(dve.scalar_tensor_tensor(out=gate.rearrange("p t e -> p (t e)"), in0=rank.rearrange("p t e -> p (t e)"),
                                          scalar=TOPK - 0.5, in1=lg.rearrange("p t e -> p (t e)"),
                                          op0=ALU.is_lt, op1=ALU.mult))
            for n in range(NB):
                qn = qkv[:, 4 * n:4 * n + 4, 0:D].unsqueeze(1).to_broadcast([P, NB, TPB, D])
                kn = qkv[:, :, D:2 * D].rearrange("p (m i) c -> p m i c", m=NB)
                link(dve.tensor_tensor(prod1.rearrange("p (m i c) -> p m i c", m=NB, i=TPB), qn, kn, ALU.mult))
                link(dve.tensor_reduce(sc[:, n, :, :].rearrange("p m x -> p (m x)"),
                                       prod1.rearrange("p (a d) -> p a d", d=DH), AX.X, ALU.add))
            link(dve.tensor_reduce(smax, sc.rearrange("p n m x -> p n x m"), AX.X, ALU.max))
            for n in range(NB):
                link(dve.tensor_tensor(sc[:, n], sc[:, n], smax[:, n, :].unsqueeze(1).to_broadcast([P, NB, TPB * H]), ALU.subtract))
            dve.sem_inc(S["pmax"], 1)
            dve.wait_ge(S["pexp"], 1)
            link(dve.tensor_reduce(ssum, pr.rearrange("p n m x -> p n x m"), AX.X, ALU.add))
            link(dve.reciprocal(ssum, ssum))
            for n in range(NB):
                link(dve.tensor_tensor(pr[:, n], pr[:, n], ssum[:, n, :].unsqueeze(1).to_broadcast([P, NB, TPB * H]), ALU.mult))
                vn = qkv[:, :, 2 * D:3 * D].rearrange("p t (h d) -> p t h d", d=DH)
                link(dve.tensor_tensor(prod1.rearrange("p (t h d) -> p t h d", t=T, h=H),
                                       pr[:, n].rearrange("p m (i h) -> p (m i) h", h=H).unsqueeze(3).to_broadcast([P, T, H, DH]),
                                       vn, ALU.mult))
                dve.tensor_reduce(attn[:, 4 * n:4 * n + 4, :].rearrange("p t c -> p (t c)"),
                                  prod1.rearrange("p (m x) -> p x m", m=NB), AX.X, ALU.add).then_inc(S["attn"], 1)
                dve.wait_ge(S["attn"], n + 1)
            for t in range(T):
                dve.wait_ge(S["moed"], t + 1)
                tmp = moe_tmp[:, t % 2, :]
                link(dve.tensor_tensor(tmp.rearrange("p (e c) -> p e c", e=E_CNT),
                                       bank[2 + t % 2][:, :, :].rearrange("p a (e c) -> p (a e) c", e=4),
                                       gate[:, t, :].unsqueeze(2).to_broadcast([P, E_CNT, D]), ALU.mult))
                dve.tensor_reduce(moe[:, t, :], tmp.rearrange("p (e c) -> p c e", e=E_CNT), AX.X, ALU.add)\
                    .then_inc(S["moes"], 1)
            for n in range(NB):
                ts = slice(4 * n, 4 * n + 4)
                dve.wait_ge(S["gth"], n + 1)
                dve.wait_ge(S["pj"], n + 1)
                m = moe[:, ts, :].rearrange("p t c -> p (t c)")
                at = attn[:, ts, :]
                link(dve.scalar_tensor_tensor(out=m, in0=th_moe[:, n, :], scalar=1.0, in1=m, op0=ALU.add, op1=ALU.mult))
                link(dve.tensor_tensor(at, B((2, 3, 0, 1)[n]).rearrange("p (t c) -> p t c", t=4),
                                       bp_row[:, :].unsqueeze(1).to_broadcast([P, 4, D]), ALU.add))
                at = at.rearrange("p t c -> p (t c)")
                link(dve.tensor_tensor(at, at, m, ALU.mult))
                xs = x[:, ts, :].rearrange("p t c -> p (t c)")
                dve.scalar_tensor_tensor(out=xs, in0=at, scalar=0.5, in1=xs, op0=ALU.mult, op1=ALU.add).then_inc(S["fin"], 1)

        @block.tensor
        def _(pe):
            pe.wait_ge(S["reach_in"], 1)
            pe.wait_ge(S["init"], 7)
            pe.matmul(B(7)[:, 0:1], ones[:, :], reach[:, :], start=True, stop=True).then_inc(S["reach"], 1)
            pe.wait_ge(in_small, 16)
            for f, what, n in fills_a:
                if f == 7:
                    pe.wait_ge(S["sd"], 1)
                    pe.wait_ge(S["xn_ready"], 1)
                if f >= 8:
                    after_a(pe, f - 8)
                if what == "w":
                    if n == 0:
                        pe.wait_ge(in_w0, 64)
                        pe.wait_ge(S["cast"], 3)
                    if n == 3:
                        pe.wait_ge(in_w1, 80)
                else:
                    pe.wait_ge(S["xn_ready"], 4 * n + 4)
                for j in range(4):
                    src = w_nat[:, 4 * n + j, :] if what == "w" else xn[:, 4 * n + j, :]
                    ins = pe.transpose(B(f % 8)[:, j * P:(j + 1) * P], src, ident)
                ins.then_inc(S["turned_a"], 1)
            for f in range(10):
                after_a(pe, f)
            pe.wait_ge(S["sigma"], 1)
            for b in range(NB):
                for blk, bk in ((WQ, 0), (WK, 1)):
                    pe.matmul(B(2 * b + bk), wT[:, blk * D:(blk + 1) * D], xnT[:, b * L:(b + 1) * L],
                              start=True, stop=True).then_inc(S["proj"], 1)
            for t in range(T):
                b8 = B(t % 8)
                if t < 8:
                    pe.wait_ge(S["part_done"], 1 + 3 * (t // 2) + (2 if t % 2 == 0 else 3))
                else:
                    pe.wait_ge(S["vt"], 2 * (t - 7))
                    pe.wait_ge(S["neg"], t - 7)
                pe.matmul(b8[:, 0:256], xnT[:, t * P:(t + 1) * P], wT[:, 0:256], start=True, stop=True)
                pe.matmul(b8[:, 256:512], xnT[:, t * P + 1:(t + 1) * P + 1], wT[:, 128:384],
                          start=True, stop=True).then_inc(S["tok"], 1)
            pe.wait_ge(S["vt"], 2 * T)
            pe.wait_ge(S["neg"], T)
            for b in range(NB):
                for k in range(3):
                    if b >= 1:
                        pe.wait_ge(S["hT"], 3 * (b - 1) + k + 1)
                    pe.matmul(B(2 * k), wT[:, (WG + k) * D:(WG + k + 1) * D], xnT[:, b * L:(b + 1) * L], start=True, stop=True)
                    pe.matmul(B(2 * k + 1), wT[:, (WU + k) * D:(WU + k + 1) * D], xnT[:, b * L:(b + 1) * L],
                              start=True, stop=True).then_inc(S["gu"], 1)
                pe.wait_ge(S["hT"], 3 * b + 3)
                if b >= 2:
                    pe.wait_ge(S["ffn_ready"], b - 1)
                for i in range(TPB):
                    for k in range(3):
                        ins = pe.matmul(B(6 + b % 2)[:, i * P:(i + 1) * P], hTt[:, k, i * P:(i + 1) * P],
                                        wT[:, (WD + k) * D:(WD + k + 1) * D], start=(k == 0), stop=(k == 2))
                ins.then_inc(S["down"], 1)

            def turn(n, h, par, half, first):
                if not first:
                    pe.wait_ge(S["g_rot"], n)
                cols = slice(half * 256, half * 256 + 256)
                wr = wr_st[:, h, :] if isinstance(h, int) else wr_st[:, bass.ds(h, 1), :].rearrange("p a n -> p (a n)")
                pe.matmul(B(6)[:, 0:256], wr[:, 0:D], qv_st[:, par, cols], start=True, stop=True)
                pe.matmul(B(6)[:, 256:512], wr[:, D:2 * D], qv_st[:, par, cols], start=True, stop=True)\
                    .then_inc(S["g_done"], 1)

            def scores(U, par, spar, i, first):
                if not first:
                    pe.wait_ge(S["maxed"], U - 1)
                main, extra = bank[par][:, 0, :], bank[par][:, 1, 0:P]
                qu = qu_st[:, spar, i * P:(i + 1) * P]
                pe.matmul(main, qu, k_st[:, spar, :], start=True, stop=False)
                pe.matmul(extra, qu, k_st[:, spar, i * P:(i + 1) * P], start=True, stop=False)
                edge = (i + 1) * P
                for n, (pg, pw) in enumerate(((0, 0), (0, 1), (1, 0))):
                    g_low = g_sb[:, spar, pg, i * P:(i + 1) * P]
                    g_up = g_sb[:, spar, pg, i * P + 1:(i + 1) * P + 1]
                    done = n == 2
                    pe.matmul(main[:, 0:edge], g_low, waves[:, 0, pw, 0:edge], start=False, stop=(done and edge == L))
                    if edge < L:
                        pe.matmul(main[:, edge:L], g_up, waves[:, 1, pw, edge:L], start=False, stop=done)
                    ins = pe.matmul(extra, g_up, waves[:, 1, pw, i * P:edge], start=False, stop=done)
                ins.then_inc(S["scored"], 1)

            def transpose(U, par, i, first):
                pe.wait_ge(S["merged"], U + 1)
                if not first:
                    pe.wait_ge(S["evaced"], U - 1)
                for c in range(TPB):
                    ins = pe.transpose(B(4 + par)[:, c * P:(c + 1) * P], prob[:, i, c * P:(c + 1) * P], ident)
                ins.then_inc(S["turned"], 1)

            def values(U, h, u, n, first):
                b, i = u // 4, u % 4
                pe.wait_ge(S["evaced"], U + 1)
                if i == 0 and not first:
                    pe.wait_ge(S["o_evac"], n)
                for c in range(TPB):
                    if isinstance(h, int):
                        v = v_parts[:, 4 * b + c, h, :]
                    else:
                        v = v_parts[:, 4 * b + c, bass.ds(h, 1), :].rearrange("p a d -> p (a d)")
                    for half in range(2):
                        ins = pe.matmul(B(7)[:, i * VW:(i + 1) * VW], probT[:, i, half, c * P:(c + 1) * P], v,
                                        start=(c == 0 and half == 0), stop=(c == TPB - 1 and half == 1))
                ins.then_inc(S["pvd"], 1)

            def head(h, first, last):
                for b in range(NB):
                    for i in range(TPB):
                        u = 4 * b + i
                        U = h * 16 + u
                        ahead = {1: 1, 3: 2}.get(i)
                        if ahead and not (last and b + ahead >= NB):
                            nb, nh = ((b + ahead) % NB, h + (b + ahead) // NB)
                            if i == 3:
                                pe.wait_ge(ldqv[nb % 2], 48 * (2 * nh + nb // 2 + 1))
                            turn(h * 8 + 2 * (b + ahead) + (i == 1), nh, nb % 2, int(i == 1), False)
                        if i == 0:
                            pe.wait_ge(S["g_ready"], h * 8 + 2 * b + 2)
                            pe.wait_ge(ld[b % 2], 96 * (2 * h + b // 2 + 1))
                        scores(U, u % 2, b % 2, i, first and u < 2)
                        if not (first and u < T_LAG):
                            transpose(U - T_LAG, (u - T_LAG) % 2, (u - T_LAG) % 4, first and u < T_LAG + 2)
                        if u >= V_LAG:
                            values(U - V_LAG, h, u - V_LAG, h * 4 + (u - V_LAG) // 4, first and u < V_LAG + 4)
                        elif not first:
                            values(U - V_LAG, h - 1, 16 - V_LAG + u, h * 4 - 1 - (V_LAG - 1 - u) // 4, False)

            pe.wait_ge(S["ffn_ready"], NB)
            pe.wait_ge(in_tab, 48)
            pe.wait_ge(ld_wr, 48)
            pe.wait_ge(ldqv[0], 48)
            pe.wait_ge(S["init"], 8)
            turn(0, 0, 0, 0, True)
            turn(1, 0, 0, 1, False)
            pe.wait_ge(ldqv[1], 48)
            turn(2, 0, 1, 0, False)
            head(0, True, False)
            with pe.Fori(1, H - 1) as h:
                head(h, False, False)
            head(H - 1, False, True)
            U = H * 16
            for k in range(V_LAG):
                u = 16 + k - V_LAG
                values(U + k - V_LAG, H - 1, u, (H - 1) * 4 + u // 4, False)
                if k < T_LAG:
                    transpose(U + k - T_LAG, (k - T_LAG) % 2, (k - T_LAG) % 4, False)
            for n in range(NB):
                pe.wait_ge(S["xn2"], 4 * n + 4)
                for i in range(4):
                    ins = pe.transpose(B(n)[:, i * P:(i + 1) * P], xn[:, 4 * n + i, :], ident)
                ins.then_inc(S["turned_b"], 1)
            for t in range(T):
                if t % 4 == 0:
                    pe.wait_ge(S["evac_b"], t // 4 + 1)
                if t >= 4:
                    pe.wait_ge(S["qkvb"], t - 3)
                else:
                    pe.wait_ge(S["evaced"], H * 16)
                    pe.wait_ge(S["o_evac"], H * NB)
                pe.matmul(B(4 + t % 4)[:, 0:QKVR], xnT[:, t * P:(t + 1) * P], wT[:, WQKV * D:], start=True, stop=True)\
                    .then_inc(S["qkvd"], 1)
            pe.wait_ge(in_w1, 80)
            for n in range(2):
                for j in range(4):
                    e = 4 * n + j
                    ins = pe.matmul(B(n)[:, j * D:(j + 1) * D], wT[:, (WI + e) * D:(WI + e + 1) * D], wo1[:, e, :],
                                    start=True, stop=True)
                ins.then_inc(S["wcd"], 1)
            pe.wait_ge(S["wcb"], 2)
            for n in range(NB):
                pe.wait_ge(S["attn"], n + 1)
                if n >= 2:
                    pe.wait_ge(S["attnTs"], n - 1)
                for i in range(4):
                    ins = pe.transpose(B(n % 2)[:, i * P:(i + 1) * P], attn[:, 4 * n + i, :], ident)
                ins.then_inc(S["attnT"], 1)
            for n in range(NB):
                pe.wait_ge(S["attnTs"], NB)
                for i in range(4):
                    t = 4 * n + i
                    ins = pe.matmul(B((2, 3, 0, 1)[n])[:, i * D:(i + 1) * D], attnT[:, t * P:(t + 1) * P],
                                    wT[:, WP * D:(WP + 1) * D], start=True, stop=True)
                ins.then_inc(S["pj"], 1)
            pe.wait_ge(S["qkvb"], T)
            for t in range(T):
                if t >= 2:
                    pe.wait_ge(S["moes"], t - 1)
                for a in range(2):
                    ins = pe.matmul(bank[2 + t % 2][:, a, :], xnT[:, t * P:(t + 1) * P],
                                    wc[:, 4 * a:4 * a + 4, :].rearrange("p e c -> p (e c)"), start=True, stop=True)
                ins.then_inc(S["moed"], 1)


_INS = ["L0_attn_w", "L0_attn_Wq", "L0_attn_Wk", "L0_attn_Wv", "L0_attn_Wr", "L0_attn_u_bias", "L0_attn_v_bias",
        "L0_ffn_w_gate", "L0_ffn_w_up", "L0_ffn_w_down", "L1_attn_Wqkv", "L1_attn_bqkv", "L1_attn_Wproj",
        "L1_attn_bproj", "L1_ffn_Wr", "L1_ffn_Wi", "L1_ffn_Wo"]


def kernel(**inputs):
    import numpy as _np
    import concourse.bacc as _bacc
    from concourse import mybir as _mybir
    from concourse.bass_utils import run_bass_kernel_spmd as _run

    nc = _bacc.Bacc("TRN2", target_bir_lowering=False, num_devices=1)
    arrays, args = {}, []
    for name, a in [(n, inputs[n]) for n in _INS] + list(tables().items()):
        a = _np.ascontiguousarray(a)
        arrays[f"in_{name}"] = a
        args.append(nc.dram_tensor(f"in_{name}", a.shape, _mybir.dt.from_np(a.dtype), kind="ExternalInput").ap())
    out = nc.dram_tensor("out", (NB, L, D), _mybir.dt.float32, kind="ExternalOutput").ap()
    build(nc, *args, out)
    r = _run(nc, [arrays], core_ids=[0])
    return r.results[0]["out"]
```

```python
from contextlib import ExitStack

import numpy as np

import concourse.bass as bass
from concourse import mybir
from concourse.alu_op_type import AluOpType as ALU

ACT = mybir.ActivationFunctionType
AX = mybir.AxisListType
F32 = mybir.dt.float32
BF16 = mybir.dt.bfloat16
F16 = mybir.dt.float16
I32 = mybir.dt.int32

P = 128
NB, L, D = 4, 512, 128
H, DH = 16, 8
TPB = L // P
T = NB * TPB
HID = 384
E_CNT, TOPK = 8, 2
SCALE = 1.0 / float(np.sqrt(np.float32(DH)))
DEQ = 1.0 / 127.0
EPS = 1e-5
BIG = 1e30
G_TOP = 2.0 ** 14
P_TOP = 2.0 ** 12
SPLITS = 3
SLOTS = 2 * SPLITS - 1
VW = SPLITS * (DH + 1)
ROWS = SPLITS * SPLITS * DH
T_LAG, LOW_LAG, V_LAG = 3, 4, 5
WIDE = L + P
WQ, WV, WK, WG, WU, WD, WI, WP, WQKV = 0, 1, 2, 3, 6, 9, 12, 20, 21
WBLOCKS = 24
QKVR = 3 * D + E_CNT
QK_DVE, PV_DVE = 2, 1
MOE_DVE = 4


def tables():
    freq = (1.0 / 10000.0 ** (np.arange(0, D, 2, dtype=np.float64) / D)).astype(np.float32).astype(np.float64)
    f = np.repeat(freq, 2)[:, None]
    odd = (np.arange(D) % 2)[:, None]

    def waves(pos):
        return np.where(odd, np.cos(f * pos), np.sin(f * pos))

    key = np.arange(L, dtype=np.float64)[None, :]
    turn = f * (key - (L - 1))
    low = waves(key)
    up = waves(key - (2 * L - 1))
    cos_t = np.cos(turn)
    sin_t = np.where(odd, -np.sin(turn), np.sin(turn))
    rot = np.stack([np.concatenate([cos_t[:, c:c + L // 2], sin_t[:, c:c + L // 2]], 1) for c in (0, L // 2)], 1)
    mask = np.zeros((P, TPB, WIDE), np.float32)
    for tile in range(TPB):
        q = tile * P + np.arange(P)[:, None]
        k = np.arange(L)[None, :]
        bad = np.where(k < (tile + 1) * P, k > q, k < q + 2)
        mask[:, tile, :L][bad] = -BIG
        kd = tile * P + np.arange(P)[None, :]
        mask[:, tile, L:][kd < q + 2] = -BIG
    tri = np.tile((np.arange(E_CNT)[None, :] < np.arange(E_CNT)[:, None]).astype(np.float32).reshape(1, -1), (P, 1))
    last = np.zeros((P, T), np.float32)
    last[P - 1, TPB - 1::TPB] = BIG
    small = np.concatenate([np.eye(P, dtype=np.float32), tri, last], 1)

    def halves(a):
        hi = a.astype(np.float16)
        return np.stack([hi, (a - hi.astype(np.float64)).astype(np.float16)], 2)

    return {
        "c_small": small,
        "c_waves": halves(np.stack([low, up], 1)),
        "c_rot": rot.astype(np.float32),
        "c_mask": mask,
    }


def build(nc, w, Wq, Wk, Wv, Wr, u_bias, v_bias, w_gate, w_up, w_down,
          Wqkv, bqkv, Wproj, bproj, Wr1, Wi, Wo, c_small, c_waves, c_rot, c_mask, out):
    ctx = ExitStack()
    with ctx:
        def sb(name, shape, dt=F32):
            return ctx.enter_context(nc.sbuf_tensor(name, shape, dt))

        def sem(name):
            return ctx.enter_context(nc.semaphore(name))

        qv_parts = nc.dram_tensor("qv_parts", (NB, H, DH, SPLITS, L), BF16, kind="Internal").ap()
        qu_parts = nc.dram_tensor("qu_parts", (NB, H, DH, SPLITS, L), BF16, kind="Internal").ap()
        k_parts = nc.dram_tensor("k_parts", (NB, H, DH, SLOTS, L), BF16, kind="Internal").ap()
        wr_parts = nc.dram_tensor("wr_parts", (DH, SLOTS, H, 2 * D), BF16, kind="Internal").ap()

        x = sb("x", [P, T, D])
        eps_col = sb("eps_col", [P, 1])
        xn = sb("xn", [P, T, D])
        xnT = sb("xnT", [P, NB * L + 1])
        stats = sb("stats", [P, T, 6])
        mean_var = sb("mean_var", [P, T, 2])
        rstd = sb("rstd", [P, T])
        w_nat = sb("w_nat", [P, WBLOCKS, D])
        w_int = sb("w_int", [P, 9, D], I32)
        wT = sb("wT", [P, WBLOCKS * D + E_CNT])
        wo1 = sb("wo1", [P, E_CNT, D])
        wr_nat = sb("wr_nat", [P, 2, D])
        wr_s = sb("wr_s", [P, SPLITS, 2 * D], BF16)
        small = sb("small", [P, P + E_CNT * E_CNT + T])
        ident = small[:, 0:P]
        tri = small[:, P:P + E_CNT * E_CNT]
        last_key = small[:, P + E_CNT * E_CNT:]
        waves = sb("waves", [P, 2, 2, L], F16)
        rot = sb("rot", [P, 2, L])
        mask = sb("mask", [P, TPB, WIDE])
        ub_col = sb("ub_col", [P, 1])
        vb_col = sb("vb_col", [P, 1])
        ub_row = sb("ub_row", [P, D])
        b_row = sb("b_row", [P, QKVR + D])
        arena = sb("arena", [P, 3 * NB * SPLITS * L // 2])
        parts = arena[:, :].bitcast(BF16).rearrange("p (a b s n) -> p a b s n", a=3, b=NB, s=SPLITS)
        qkv = arena[:, 0:T * QKVR].rearrange("p (t c) -> p t c", t=T)
        rest = sb("rest", [P, 2, L])
        v_parts = sb("v_parts", [P, T, H, VW], BF16)
        norms = sb("norms", [P, 2])
        reach = sb("reach", [P, 1])
        sigma = sb("sigma", [P, 1])
        scale_neg = sb("scale_neg", [P, 1])
        ones = sb("ones", [P, P])
        v_next = sb("v_next", [P, T, D])
        neg_s = sb("neg_s", [P, H + 1, T])
        shift = sb("shift", [P, H, T])
        ffn = sb("ffn", [P, T, D])
        o_all = sb("o_all", [P, T, H, DH + 1])
        qu_st = sb("qu_st", [ROWS, 2, L], BF16)
        qv_st = sb("qv_st", [ROWS, 2, L], BF16)
        k_st = sb("k_st", [ROWS, 2, L], BF16)
        wr_st = sb("wr_st", [ROWS, H, 2 * D], BF16)
        work = sb("work", [P, 7680])

        def area(at, *shape):
            n = int(np.prod(shape))
            names = "abcd"[:len(shape)]
            return work[:, at:at + n].rearrange(f"p ({' '.join(names)}) -> p {' '.join(names)}",
                                                **dict(zip(names, shape)))

        turned_g = arena[:, 0:2 * L].rearrange("p (a n) -> p a n", a=2)
        g_sum = arena[:, 2 * L:3 * L].rearrange("p (a n) -> p a n", a=2)
        s_sb = area(1536, 4, WIDE)
        prob = arena[:, 6656:6656 + 4 * WIDE].rearrange("p (a n) -> p a n", a=4)
        probT = area(4096, 4, L).bitcast(F16).rearrange("p a (s n) -> p a s n", s=2)
        g_sb = arena[:, 3 * L:5 * L + 4].bitcast(F16).rearrange("p (a s n) -> p a s n", a=2, s=2)
        start = sb("start", [P, T])
        shift_now = sb("shift_now", [P, T])
        pace = sb("pace", [P, 2])

        bank = [ctx.enter_context(nc.psum_tensor(f"bank{i}", [P, 2, 512], F32)) for i in range(4)]

        def B(i):
            return bank[i // 2][:, i % 2, :]

        in_x = [sem(f"in_x{i}") for i in range(2)]
        in_w0, in_wint, in_w1, in_small, in_tab, in_bias, in_b1 = (
            sem(n) for n in ("in_w0", "in_wint", "in_w1", "in_small", "in_tab", "in_bias", "in_b1"))
        block = ctx.enter_context(nc.Block())

        S = {n: sem(n) for n in ("fill_out_v", "fill_out_a", "g_done", "scored", "wr_split", "wr_written",
            "scratch_written", "v_out", "v_moved", "result_ready", "stored", "preset", "pool_order", "norm_in",
            "swap", "ints_cast", "part2", "part3_p", "v_split", "v_rest", "v_two", "part3_v", "x_high", "x_low",
            "bias_rows", "g_rot", "g_sum", "g_ready", "exped", "merged", "e1", "den", "gate_over", "next_share",
            "qkv_out", "product_used", "product", "probs", "experts_gated", "moe_part", "moe_own", "moe_ready",
            "norm", "variance", "deviation", "fill_turned", "projected", "part1", "rest_ready", "sigma",
            "weights_turned", "weights_out", "w16", "tokens_done", "next_product", "gate_up_done", "hidden_ready",
            "gate_tanh", "down_done", "ffn_ready", "out_tanh", "turned", "sums_done", "hi_done", "maxed", "e1_in",
            "expert_weights", "expert_weights_out", "x2_ready", "deviation1", "norm_factors", "xn1_ready",
            "xn1_turned", "xn1_out", "qkv_done", "logits_shifted", "logits_exp", "scores1_shifted", "scores1_exp",
            "gate", "experts_done", "attn_turned", "attn_turned_out", "moe_tanh", "dve_order", "stats_done",
            "xn_ready", "reach_in", "reach", "q_u", "hidden_gate", "sums_out", "low_done", "attn_projected")}
        ld = [sem(f"ld{i}") for i in range(2)]
        ldqv = [sem(f"ldqv{i}") for i in range(2)]
        ld_wr = sem("ld_wr")

        xr = w.rearrange("b (i p) c -> p (b i) c", p=P)
        outr = out.rearrange("b (i p) c -> p (b i) c", p=P)
        FILLS = 5
        dve_fills, act_fills = (1, 3), (0, 2, 4)

        def after_part3(eng, n):
            eng.wait_ge(S["part3_v" if n % 2 else "part3_p"], n // 2 + 1)

        def after_fill(eng, f):
            if f in dve_fills:
                eng.wait_ge(S["fill_out_v"], dve_fills.index(f) + 1)
            else:
                eng.wait_ge(S["fill_out_a"], act_fills.index(f) + 1)

        prod0 = area(0, T, D)
        s_next = work[:, 2304:2560]
        th = area(2560, 3, L)
        q_u = area(2048, 2, D)
        hg = [area(4096, L), area(4096 + L, L), area(1536, L)]
        rests = [rest[:, 0, :], rest[:, 1, :], area(4096, L), area(4096 + L, L), area(2560, L)]
        hidden = [area(5120, 3, L), area(0, 3, L)]
        th2 = area(6656, 2, L)
        x16 = xn[:, :, :].rearrange("p t c -> p (t c)").bitcast(F16).rearrange("p (s n) -> p s n", s=2)
        w16 = w_nat[:, WG:WG + 3, :].rearrange("p a c -> p (a c)").bitcast(F16)
        v_all = o_all[:, :, :, :].rearrange("p t h d -> p (t h d)")[:, 0:T * D].rearrange("p (t c) -> p t c", t=T)
        def group(a, i):
            return a[:, i::TPB]

        e1d = work[:, 0:H * T]
        e1 = work[:, 256:256 + H * T]
        den = area(512, T, H)
        num = area(768, TPB, NB, D)
        sc = area(2816, TPB, NB, NB * H)
        pr = area(3840, TPB, NB, NB * H)
        smax = area(4864, TPB, NB * H)
        ssum = area(5120, TPB, NB * H)
        gate = area(5376, TPB, NB, E_CNT)
        rank = area(5504, TPB, NB * E_CNT)
        rsum = area(5632, TPB, NB)
        lg = area(5648, TPB, NB, E_CNT)
        gt = area(5776, NB, E_CNT * E_CNT)
        eq = area(6032, NB, E_CNT * E_CNT)
        gated = area(6288, 2, (E_CNT - MOE_DVE) * D)
        offset = sb("offset", [P, T])
        products = [mask[:, :, :].rearrange("p a n -> p (a n)")[:, 0:NB * NB * D],
                    w_nat[:, E_CNT:, :].rearrange("p a n -> p (a n)")]

        def moe_bank(k):
            return bank[1 + k % 3]

        def qk_product(eng, k, i, lo, hi):
            room = products[k % 2][:, lo * NB * D:hi * NB * D]
            shape = [P, hi - lo, NB, D]
            return eng.tensor_tensor(room.rearrange("p (n m c) -> p n m c", n=hi - lo, m=NB),
                                     group(qkv, i)[:, lo:hi, 0:D].unsqueeze(2).to_broadcast(shape),
                                     group(qkv, i)[:, :, D:2 * D].unsqueeze(1).to_broadcast(shape), ALU.mult)

        def pv_product(eng, k, i, n):
            return eng.tensor_tensor(
                products[k % 2][:, n * NB * D:(n + 1) * NB * D].rearrange("p (m h d) -> p m h d", m=NB, h=H),
                pr[:, i, n].rearrange("p (m h) -> p m h", m=NB).unsqueeze(3).to_broadcast([P, NB, H, DH]),
                group(qkv, i)[:, :, 2 * D:3 * D].rearrange("p m (h d) -> p m h d", h=H), ALU.mult)

        attn = v_next
        attnT = ffn[:, :, :].rearrange("p t c -> p (t c)")
        moe = xn
        th_moe = o_all[:, :, :, :].rearrange("p t h d -> p (t h d)")[:, 0:T * D].rearrange("p (n c) -> p n c", n=NB)
        wc = w_nat[:, 0:E_CNT, :]
        BIASES = QKVR + D
        bias_room = w_int[:, :, :].rearrange("p a n -> p (a n)").bitcast(BF16)
        bias_split = [bias_room[:, k * BIASES:(k + 1) * BIASES] for k in range(SPLITS)]
        bias_rows = bias_room[:, SPLITS * BIASES:(SPLITS + 1) * BIASES]
        ones_rows = bias_room[:, (SPLITS + 1) * BIASES:(SPLITS + 1) * BIASES + P]

        @block.sync
        def _(sp):
            sp.dma_start(x[:, 0:8, :], xr[:, 0:8, :]).then_inc(in_x[0], 16)
            sp.dma_start(w_nat[:, WQ, :], Wq).then_inc(in_w0, 16)
            sp.dma_start(w_nat[:, WV, :], Wv).then_inc(in_w0, 16)
            sp.dma_start(w_nat[:, WK, :], Wk).then_inc(in_w0, 16)
            sp.dma_start(wr_nat[:, 0, :], Wr).then_inc(in_w0, 16)
            sp.dma_start(x[:, 8:16, :], xr[:, 8:16, :]).then_inc(in_x[1], 16)
            sp.dma_start(waves[:, :, :], c_waves).then_inc(in_tab, 16)
            sp.dma_start(rot[:, :, :], c_rot).then_inc(in_tab, 16)
            sp.dma_start(mask[:, :, :], c_mask).then_inc(in_tab, 16)
            sp.dma_start(w_nat[:, WI:WI + E_CNT, :], Wi.rearrange("e d h -> d e h")).then_inc(in_w1, 16)
            sp.dma_start(w_nat[:, WP, :], Wproj).then_inc(in_w1, 16)
            sp.dma_start(w_nat[:, WQKV:WQKV + 3, :], Wqkv.rearrange("(k p) c -> p k c", p=P)).then_inc(in_w1, 16)
            sp.dma_start(wT[:, WBLOCKS * D:], Wr1).then_inc(in_w1, 16)
            sp.dma_start(wo1[:, :, :], Wo.rearrange("e h d -> h e d")).then_inc(in_w1, 16)

            def piece(scr, h, b, lo, hi):
                at = scr[b, h:h + 1] if isinstance(h, int) else scr[b, bass.ds(h, 1)]
                return at[:, :, lo:hi].rearrange("a d s n -> (a d) s n")

            def load_qv(h, b, base):
                if base is not None:
                    sp.wait_ge(S["g_done"], base)
                for r in range(SPLITS):
                    rows = slice(r * SPLITS * DH, (r + 1) * SPLITS * DH)
                    sp.dma_start(qv_st[rows, b % 2, :], piece(qv_parts, h, b, 0, 3)).then_inc(ldqv[b % 2], 16)

            def load_quk(h, b, base):
                if base is not None:
                    sp.wait_ge(S["scored"], base)
                for r in range(SPLITS):
                    rows = slice(r * SPLITS * DH, (r + 1) * SPLITS * DH)
                    sp.dma_start(qu_st[rows, b % 2, :], piece(qu_parts, h, b, 0, 3)).then_inc(ld[b % 2], 16)
                    sp.dma_start(k_st[rows, b % 2, :], piece(k_parts, h, b, r, r + 3)).then_inc(ld[b % 2], 16)

            sp.wait_ge(S["wr_split"], 1)
            for s in range(SLOTS):
                sp.dma_start(wr_parts[:, s].rearrange("d h n -> h d n"), wr_s[:, s % 3, :]).then_inc(S["wr_written"], 16)
            for b in range(NB):
                for kind, scr in enumerate((qv_parts, qu_parts, k_parts)):
                    after_part3(sp, 3 * b + kind)
                    sp.dma_start(scr[b].rearrange("h d s n -> (h d) s n")[:, 0:SPLITS],
                                 parts[:, kind, b]).then_inc(S["scratch_written"], 16)
                sp.dma_start(k_parts[b].rearrange("h d s n -> (h d) s n")[:, SPLITS:],
                             parts[:, 2, b, 0:SPLITS - 1]).then_inc(S["scratch_written"], 16)
            sp.wait_ge(S["wr_written"], 16 * SLOTS)
            for r in range(SPLITS):
                rows = slice(r * SPLITS * DH, (r + 1) * SPLITS * DH)
                sp.dma_start(wr_st[rows, :, :].rearrange("a h n -> a (h n)"),
                             wr_parts[:, r:r + 3].rearrange("d s h n -> d s (h n)")).then_inc(ld_wr, 16)
            sp.wait_ge(S["v_out"], T)
            sp.dma_start(v_next[0:P - 1, :, :], v_all[1:P, :, :]).then_inc(S["v_moved"], 16)
            sp.dma_start(v_next[P - 1:P, 0:T - 1, :], v_all[0:1, 1:T, :]).then_inc(S["v_moved"], 16)
            sp.dma_start(v_next[P - 1:P, T - 1, :], v_all[0:1, 0, :]).then_inc(S["v_moved"], 16)
            sp.wait_ge(S["scratch_written"], 16 * NB * 4)
            for b in range(NB):
                load_qv(0, b, 2 * (b - 1) if b >= 2 else None)
                if b >= 1:
                    load_quk(0, b - 1, 4 * (b - 2) if b >= 3 else None)
            with sp.Fori(1, H) as h:
                for b in range(NB):
                    load_qv(h, b, h * 8 + 2 * (b - 1))
                    if b == 0:
                        load_quk(h - 1, NB - 1, h * 16 - 8)
                    else:
                        load_quk(h, b - 1, h * 16 + 4 * (b - 2))
            load_quk(H - 1, NB - 1, H * 16 - 8)
            for i in range(TPB):
                sp.wait_ge(S["result_ready"], i + 1)
                sp.dma_start(group(outr, i), group(x, i)).then_inc(S["stored"], 16)
            sp.wait_ge(S["stored"], 16 * TPB)

        @block.gpsimd
        def _(pool):
            pool.memset(eps_col[:, :], EPS).then_inc(S["preset"], 1)
            pool.memset(b_row[:, 3 * D:QKVR], 0.0).then_inc(S["preset"], 1)
            pool.memset(xnT[:, NB * L:], 0.0).then_inc(S["preset"], 1)
            pool.memset(ones[:, :], 1.0).then_inc(S["preset"], 1)
            pool.memset(v_parts[:, :, :, DH:DH + 1], 1.0).then_inc(S["preset"], 1)
            pool.memset(v_parts[:, :, :, 2 * DH + 1:2 * DH + 2], 0.0).then_inc(S["preset"], 1)
            pool.memset(v_parts[:, :, :, 3 * DH + 2:], 0.0).then_inc(S["preset"], 1)
            pool.dma_start(b_row[:, 0:3 * D], bqkv.partition_broadcast(P)).then_inc(in_b1, 16)
            pool.dma_start(b_row[:, QKVR:], bproj.partition_broadcast(P)).then_inc(in_b1, 16)
            order = [0]

            def done(ins):
                order[0] += 1
                ins.then_inc(S["pool_order"], 1)
                pool.wait_ge(S["pool_order"], order[0])

            pool.wait_ge(in_w0, 64)
            pair = wr_nat[:, 0, :].rearrange("p (k two) -> p k two", two=2)
            swap = wr_nat[:, 1, :].rearrange("p (k two) -> p k two", two=2)
            pool.wait_ge(S["norm_in"], 2)
            pool.tensor_copy(swap[:, :, 0], pair[:, :, 1]).then_inc(S["swap"], 1)
            pool.tensor_copy(swap[:, :, 1], pair[:, :, 0]).then_inc(S["swap"], 1)
            pool.wait_ge(S["swap"], 2)
            both = wr_nat[:, :, :].rearrange("p a c -> p (a c)")
            done(pool.tensor_copy(wr_s[:, 0, :], both))
            done(pool.tensor_tensor(both, both, wr_s[:, 0, :], ALU.subtract))
            done(pool.tensor_copy(wr_s[:, 1, :], both))
            pool.tensor_tensor(wr_s[:, 2, :], both, wr_s[:, 1, :], ALU.subtract).then_inc(S["wr_split"], 1)
            pool.wait_ge(in_wint, 48)
            for k in range(3):
                pool.tensor_copy(w_nat[:, WG + 3 * k:WG + 3 * k + 3, :], w_int[:, 3 * k:3 * k + 3, :]).then_inc(S["ints_cast"], 1)

            for n in range(0, 3 * NB, 2):
                pool.wait_ge(S["part2"], n + 1)
                pool.tensor_tensor(parts[:, n % 3, n // 3, 2, :], rests[n % 5], parts[:, n % 3, n // 3, 1, :],
                                   ALU.subtract).then_inc(S["part3_p"], 1)

            def value_rest(b):
                pool.wait_ge(S["v_out"], TPB * b + TPB)
                if b >= 2:
                    pool.wait_ge(S["v_split"], b - 1)
                pool.tensor_tensor(rest[:, b % 2, :].rearrange("p (t h d) -> p t h d", t=TPB, h=H),
                                   v_all[:, TPB * b:TPB * b + TPB, :].rearrange("p t (h d) -> p t h d", h=H),
                                   v_parts[:, TPB * b:TPB * b + TPB, :, 0:DH], ALU.subtract).then_inc(S["v_rest"], 1)

            def value_third(b):
                pool.wait_ge(S["v_two"], b + 1)
                ts = slice(TPB * b, TPB * b + TPB)
                at = 2 * (DH + 1)
                pool.tensor_tensor(v_parts[:, ts, :, at:at + DH],
                                   rest[:, b % 2, :].rearrange("p (t h d) -> p t h d", t=TPB, h=H),
                                   v_parts[:, ts, :, DH + 1:2 * DH + 1], ALU.subtract).then_inc(S["v_split"], 1)

            pool.wait_ge(S["part3_v"], 3 * NB // 2)
            pool.wait_ge(S["part3_p"], 3 * NB // 2)
            for b in range(NB):
                cols = slice(b * L, (b + 1) * L)
                pool.wait_ge(S["x_high"], b + 1)
                pool.tensor_tensor(x16[:, 1, cols], xnT[:, cols], x16[:, 0, cols], ALU.subtract).then_inc(S["x_low"], 1)
                value_rest(b)
                if b:
                    value_third(b - 1)
            value_third(NB - 1)
            pool.wait_ge(in_b1, 32)
            pool.wait_ge(S["preset"], 7)
            pool.wait_ge(S["ints_cast"], 3)
            zero = ones_rows
            done(pool.memset(bias_rows, 0.0))
            done(pool.memset(zero, 0.0))
            for k in range(SPLITS):
                zeros = zero[:, 0:1].to_broadcast([P, BIASES])
                done(pool.tensor_tensor(bias_split[k], b_row[:, :], zeros, ALU.add))
                if k < SPLITS - 1:
                    done(pool.tensor_tensor(b_row[:, :], b_row[:, :], bias_split[k], ALU.subtract))
                row = slice(32 * k, 32 * k + 1)
                done(pool.tensor_tensor(bias_rows[row, :], bias_split[k][row, :], zeros[row, :], ALU.add))
            pool.memset(ones_rows, 1.0).then_inc(S["bias_rows"], 1)

            def rotate(n, par, half, free):
                pool.wait_ge(S["g_rot"], n + 1)
                if free is not None:
                    pool.wait_ge(S["scored"], free)
                cols = slice(half * 256, half * 256 + 256)
                pool.tensor_tensor(g_sum[:, half, :], turned_g[:, half, 0:256], turned_g[:, half, 256:512],
                                   ALU.add).then_inc(S["g_sum"], 1)
                pool.tensor_tensor(g_sb[:, par, 0, cols], turned_g[:, half, 0:256], turned_g[:, half, 256:512],
                                   ALU.add).then_inc(S["g_sum"], 1)
                pool.wait_ge(S["g_sum"], 2 * n + 2)
                pool.tensor_tensor(g_sb[:, par, 1, cols], g_sum[:, half, :], g_sb[:, par, 0, cols],
                                   ALU.subtract).then_inc(S["g_ready"], 1)

            def merge(U, i):
                pool.wait_ge(S["exped"], U + 1)
                cols = slice(i * P, i * P + P)
                pool.tensor_tensor(prob[:, i, cols], prob[:, i, cols], prob[:, i, L:WIDE],
                                   ALU.add).then_inc(S["merged"], 1)

            def head(h, first, last):
                for b in range(NB):
                    for i in range(TPB):
                        ahead = {1: 1, 3: 2}.get(i)
                        if ahead and not (last and b + ahead >= NB):
                            free = None if first and b + ahead < 2 else h * 16 + 4 * (b + ahead - 1)
                            rotate(h * 8 + 2 * (b + ahead) + (i == 1), (b + ahead) % 2, int(i == 1), free)
                        merge(h * 16 + 4 * b + i, i)

            pool.wait_ge(ldqv[0], 48)
            pool.memset(g_sb[:, :, :, L:], 0.0).then_inc(S["preset"], 1)
            rotate(0, 0, 0, None)
            rotate(1, 0, 1, None)
            rotate(2, 1, 0, None)
            head(0, True, False)
            with pool.Fori(1, H - 1) as h:
                head(h, False, False)
            head(H - 1, False, True)

            e1v = e1.rearrange("p (h t) -> p t h", h=H)
            pool.wait_ge(S["e1"], 2)
            for i in range(TPB):
                if i == 2:
                    pool.wait_ge(S["den"], 1)
                    for j in (2, 3):
                        f = group(ffn, j).rearrange("p n (h d) -> p n h d", h=H)
                        pool.tensor_tensor(f, f, group(den, j).unsqueeze(3).to_broadcast([P, NB, H, DH]), ALU.mult)\
                            .then_inc(S["gate_over"], 1)
                pool.tensor_tensor(num[:, i].rearrange("p n (h d) -> p n h d", h=H),
                                   group(v_next, i).rearrange("p n (h d) -> p n h d", h=H),
                                   group(e1v, i).unsqueeze(3).to_broadcast([P, NB, H, DH]), ALU.mult).then_inc(S["next_share"], 1)

            def score_products(k, i):
                pool.wait_ge(S["qkv_out"], NB * (i + 1))
                if k >= 2:
                    pool.wait_ge(S["product_used"], k - 1)
                qk_product(pool, k, i, 0, NB - QK_DVE).then_inc(S["product"], 1)

            def value_products(k, i):
                pool.wait_ge(S["probs"], i + 1)
                pool.wait_ge(S["product_used"], k - 1)
                for n in range(NB - PV_DVE):
                    ins = pv_product(pool, k, i, n)
                ins.then_inc(S["product"], 1)

            def expert_sums(i, tiles):
                for n in tiles:
                    k = NB * i + n
                    half = 2 * D
                    tmp = gated[:, k % 2, :]
                    pool.wait_ge(S["experts_gated"], k + 1)
                    done(pool.tensor_tensor(tmp[:, 0:half], tmp[:, 0:half], tmp[:, half:2 * half], ALU.add))
                    pool.tensor_tensor(num[:, i, n, :], tmp[:, 0:D], tmp[:, D:2 * D], ALU.add).then_inc(S["moe_part"], 1)
                if tiles[-1] == NB - 1:
                    pool.wait_ge(S["moe_part"], NB * i + NB)
                    pool.wait_ge(S["moe_own"], NB * i + NB)
                    pool.tensor_tensor(group(moe, i), group(moe, i), num[:, i], ALU.add).then_inc(S["moe_ready"], 1)

            first, second = (0, 1), (2, 3)
            score_products(0, 0)
            score_products(1, 1)
            value_products(2, 0)
            expert_sums(0, first)
            score_products(3, 2)
            expert_sums(0, second)
            value_products(4, 1)
            expert_sums(1, first)
            score_products(5, 3)
            expert_sums(1, second)
            value_products(6, 2)
            expert_sums(2, first)
            expert_sums(2, second)
            value_products(7, 3)
            expert_sums(3, first)
            expert_sums(3, second)

        @block.scalar
        def _(act):
            act.dma_start(small[:, :], c_small).then_inc(in_small, 16)
            act.dma_start(vb_col[:, :], v_bias.rearrange("h (d o) -> (h d) o", o=1)).then_inc(in_bias, 16)
            act.dma_start(ub_col[:, :], u_bias.rearrange("h (d o) -> (h d) o", o=1)).then_inc(in_bias, 16)
            act.dma_start(ub_row[:, :], u_bias.rearrange("h d -> (h d)").partition_broadcast(P)).then_inc(in_bias, 16)
            act.dma_start(w_int[:, 0:3, :], w_gate.rearrange("(k p) c -> p k c", p=P)).then_inc(in_wint, 16)
            act.dma_start(w_int[:, 3:6, :], w_up.rearrange("(k p) c -> p k c", p=P)).then_inc(in_wint, 16)
            act.dma_start(w_int[:, 6:9, :], w_down.rearrange("d (k h) -> d k h", k=3)).then_inc(in_wint, 16)
            act.wait_ge(S["preset"], 7)
            act.wait_ge(S["norm_in"], 2)
            act.activation(norms[:, :], norms[:, :], ACT.Sqrt).then_inc(S["norm"], 1)
            act.wait_ge(S["variance"], T)
            act.activation(rstd[:, :], mean_var[:, :, 1], ACT.Sqrt, bias=eps_col[:, 0:1]).then_inc(S["deviation"], 1)
            for f in act_fills:
                act.wait_ge(S["fill_turned"], f + 1)
                dst = wT[:, 0:L] if f == 0 else xnT[:, (f - 1) * L:f * L]
                act.activation(dst, B(f), ACT.Copy).then_inc(S["fill_out_a"], 1)
            def x_high(b):
                cols = slice(b * L, (b + 1) * L)
                after_fill(act, b + 1)
                act.wait_ge(S["fill_turned"], FILLS)
                act.activation(x16[:, 0, cols], xnT[:, cols], ACT.Copy).then_inc(S["x_high"], 1)

            def value_second(b):
                act.wait_ge(S["v_rest"], b + 1)
                act.activation(v_parts[:, TPB * b:TPB * b + TPB, :, DH + 1:2 * DH + 1],
                               rest[:, b % 2, :].rearrange("p (t h d) -> p t h d", t=TPB, h=H), ACT.Copy)\
                    .then_inc(S["v_two"], 1)

            def part1(n):
                b, kind = n // 3, n % 3
                act.wait_ge(S["projected"], 2 * b + (1 if kind < 2 else 2))
                src = B(2 * b + (kind == 2))
                if kind < 2:
                    act.activation(parts[:, kind, b, 0, :], src, ACT.Identity,
                                   bias=(vb_col, ub_col)[kind][:, 0:1]).then_inc(S["part1"], 1)
                else:
                    act.activation(parts[:, kind, b, 0, :], src, ACT.Copy).then_inc(S["part1"], 1)

            def part2(n):
                act.wait_ge(S["rest_ready"], n + 1)
                act.activation(parts[:, n % 3, n // 3, 1, :], rests[n % 5], ACT.Copy).then_inc(S["part2"], 1)

            act.wait_ge(S["sigma"], 1)
            for n in range(3 * NB + 2):
                if n < 3 * NB:
                    part1(n)
                if n >= 2:
                    part2(n - 2)
            for k in range(2):
                act.wait_ge(S["weights_turned"], k + 1)
                act.activation(wT[:, (k + 1) * L:(k + 2) * L], B(k), ACT.Copy).then_inc(S["weights_out"], 1)
            act.wait_ge(S["weights_out"], 2)
            act.activation(w16, wT[:, WG * D:(WG + 6) * D], ACT.Copy).then_inc(S["w16"], 1)
            for t in range(T):
                act.wait_ge(S["tokens_done"], t + 1)
                act.wait_ge(S["next_product"], t + 1)
                src = B(2 + t % 6)[:, D:2 * D]
                act.activation(v_all[:, t, :], src, ACT.Copy)
                act.activation(v_parts[:, t, :, 0:DH], src.rearrange("p (h d) -> p h d", h=H), ACT.Copy).then_inc(S["v_out"], 1)
                if t % TPB == 1:
                    x_high(t // TPB)
                if t % TPB == 2 and t > TPB:
                    value_second(t // TPB - 1)
            value_second(NB - 1)
            for k in range(2, 5):
                act.wait_ge(S["weights_turned"], k + 1)
                act.activation(wT[:, (k + 1) * L:(k + 2) * L], B(6 + k % 2), ACT.Copy).then_inc(S["weights_out"], 1)

            def gate_tanh(j):
                act.wait_ge(S["gate_up_done"], j + 1)
                if j >= 3:
                    act.wait_ge(S["hidden_ready"], j - 2)
                act.activation(th[:, j % 3, :], B(2 * (j % 3)), ACT.Tanh, scale=DEQ / 2).then_inc(S["gate_tanh"], 1)

            def out_tanh(b):
                act.wait_ge(S["down_done"], b + 1)
                if b >= 2:
                    act.wait_ge(S["ffn_ready"], b - 1)
                act.activation(th2[:, b % 2, :], B(7), ACT.Tanh, scale=DEQ ** 3 / 4).then_inc(S["out_tanh"], 1)

            for j in range(3 * NB):
                gate_tanh(j)
                if j >= 6 and j % 3 == 0:
                    out_tanh(j // 3 - 2)
            out_tanh(NB - 2)
            out_tanh(NB - 1)

            def high_half(U, u, first):
                act.wait_ge(S["turned"], U + 1)
                if not first:
                    act.wait_ge(S["sums_done"], U - 3)
                act.activation(probT[:, u % 4, 0, :], B(4 + u % 2), ACT.Copy, scale=P_TOP).then_inc(S["hi_done"], 1)

            def row(a, h, lo, hi):
                if isinstance(h, int):
                    return a[:, h, lo:hi]
                return a[:, bass.ds(h, 1), lo:hi].rearrange("p a c -> p (a c)")

            def head(h, first):
                for b in range(NB):
                    for i in range(TPB):
                        u = 4 * b + i
                        U = h * 16 + u
                        if not (first and u < T_LAG):
                            high_half(U - T_LAG, (u - T_LAG) % 4, first and u < T_LAG + 4)
                        if u == 2:
                            act.activation(start[:, T // 2:], row(neg_s, h, T // 2, T), ACT.Copy)
                        if u == 8:
                            act.activation(row(shift, h, 0, T // 2), shift_now[:, 0:T // 2], ACT.Copy)
                        if u == 11:
                            act.activation(start[:, 0:T // 2], row(neg_s, h + 1, 0, T // 2), ACT.Copy)
                        act.wait_ge(S["maxed"], U + 1)
                        if not (first and u < 4):
                            act.wait_ge(S["turned"], U - 3)
                        act.activation(prob[:, i, :], s_sb[:, i, :], ACT.Exp, bias=shift_now[:, u:u + 1],
                                       scale=-1.0).then_inc(S["exped"], 1)
                act.activation(row(shift, h, T // 2, T), shift_now[:, T // 2:], ACT.Copy)

            head(0, True)
            with act.Fori(1, H) as h:
                head(h, False)
            for back in range(T_LAG, 0, -1):
                high_half(H * 16 - back, -back % 4, False)
            act.wait_ge(S["e1_in"], 1)
            act.activation(e1d, e1d, ACT.Exp).then_inc(S["e1"], 1)
            act.wait_ge(S["e1"], 1)
            act.activation(e1, e1d, ACT.Copy, scale=P_TOP).then_inc(S["e1"], 1)
            for n in range(2):
                act.wait_ge(S["expert_weights"], n + 1)
                act.activation(wc[:, 4 * n:4 * n + 4, :].rearrange("p e c -> p (e c)"), B(n), ACT.Copy).then_inc(S["expert_weights_out"], 1)

            def deviations(g):
                act.wait_ge(S["x2_ready"], g + 1)
                both = slice(g, g + 1 if g < 2 else TPB)
                act.activation(rstd[:, :].rearrange("p (n i) -> p n i", i=TPB)[:, :, both],
                               mean_var[:, :, 1].rearrange("p (n i) -> p n i", i=TPB)[:, :, both],
                               ACT.Sqrt, bias=eps_col[:, 0:1]).then_inc(S["deviation1"], 1)

            def normed(i):
                act.wait_ge(S["norm_factors"], min(i, 2) + 1)
                for t in range(i, T, TPB):
                    act.activation(xn[:, t, :], x[:, t, :], ACT.Identity, scale=rstd[:, t:t + 1],
                                   bias=offset[:, t:t + 1]).then_inc(S["xn1_ready"], 1)

            def xnT_out(i):
                act.wait_ge(S["xn1_turned"], i + 1)
                act.activation(group(xnT[:, 0:NB * L].rearrange("p (t c) -> p t c", c=P), i),
                               B(i % 2).rearrange("p (n c) -> p n c", c=P), ACT.Copy).then_inc(S["xn1_out"], 1)

            def qkv_out(i):
                for n in range(NB):
                    k = NB * i + n
                    act.wait_ge(S["qkv_done"], k + 1)
                    act.activation(qkv[:, TPB * n + i, :], B(2 + k % 2)[:, 0:QKVR], ACT.Copy).then_inc(S["qkv_out"], 1)

            def router_exp(i):
                act.wait_ge(S["logits_shifted"], i + 1)
                act.activation(lg[:, i], lg[:, i], ACT.Exp).then_inc(S["logits_exp"], 1)

            def score_exp(i):
                act.wait_ge(S["scores1_shifted"], i + 1)
                act.activation(pr[:, i], sc[:, i], ACT.Exp, scale=SCALE).then_inc(S["scores1_exp"], 1)

            def gate_experts(i, tiles):
                act.wait_ge(S["gate"], i + 1)
                for n in tiles:
                    k = NB * i + n
                    act.wait_ge(S["experts_done"], k + 1)
                    if k >= 2:
                        act.wait_ge(S["moe_part"], k - 1)
                    for e in range(MOE_DVE, E_CNT):
                        at = (e - MOE_DVE) * D
                        ins = act.activation(gated[:, k % 2, at:at + D], moe_bank(k)[:, 1, at:at + D], ACT.Copy,
                                             scale=gate[:, i, n, e:e + 1])
                    ins.then_inc(S["experts_gated"], 1)

            def attnT_out(i):
                act.wait_ge(S["attn_turned"], i + 1)
                act.activation(attnT[:, i * L:(i + 1) * L], B(0), ACT.Copy).then_inc(S["attn_turned_out"], 1)

            def moe_tanh(i):
                act.wait_ge(S["moe_ready"], i + 1)
                act.activation(th_moe[:, i, :].rearrange("p (n c) -> p n c", n=NB), group(moe, i), ACT.Tanh,
                               scale=0.5).then_inc(S["moe_tanh"], 1)

            deviations(0)
            normed(0)
            xnT_out(0)
            deviations(1)
            normed(1)
            qkv_out(0)
            xnT_out(1)
            deviations(2)
            router_exp(0)
            normed(2)
            qkv_out(1)
            normed(3)
            xnT_out(2)
            xnT_out(3)
            router_exp(1)
            qkv_out(2)
            score_exp(0)
            qkv_out(3)
            first, second = (0, 1), (2, 3)
            gate_experts(0, first)
            score_exp(1)
            gate_experts(0, second)
            for i in range(2, TPB):
                router_exp(i)
                attnT_out(i - 2)
                gate_experts(i - 1, first)
                moe_tanh(i - 2)
                score_exp(i)
                gate_experts(i - 1, second)
            attnT_out(2)
            gate_experts(3, first)
            moe_tanh(2)
            gate_experts(3, second)
            moe_tanh(3)
            attnT_out(3)

        @block.vector
        def _(dve):
            c = [0]

            def mark(ins):
                c[0] += 1
                ins.then_inc(S["dve_order"], 1)
                return c[0]

            def after(k):
                dve.wait_ge(S["dve_order"], k)

            def link(ins):
                after(mark(ins))

            dve.wait_ge(in_x[0], 16)
            for t in range(T):
                if t == 8:
                    dve.wait_ge(in_w0, 64)
                    for k, src in enumerate((w_nat[:, WQ, :], wr_nat[:, 0, :])):
                        dve.tensor_tensor_reduce(rest[:, k, 0:D], src, src, 1.0, 0.0, ALU.mult, ALU.add,
                                                 norms[:, k:k + 1]).then_inc(S["norm_in"], 1)
                    dve.wait_ge(in_x[1], 16)
                dve.bn_stats(stats[:, t, :], x[:, t, :]).then_inc(S["stats_done"], 1)
            for t in range(T):
                dve.wait_ge(S["stats_done"], t + 1)
                dve.bn_aggr(mean_var[:, t, :], stats[:, t, :]).then_inc(S["variance"], 1)
            dve.wait_ge(S["deviation"], 1)
            link(dve.reciprocal(rstd[:, :], rstd[:, :]))
            for t in range(T):
                dve.tensor_scalar(xn[:, t, :], x[:, t, :], mean_var[:, t, 0:1], rstd[:, t:t + 1],
                                  ALU.subtract, ALU.mult).then_inc(S["xn_ready"], 1)
            dve.wait_ge(in_bias, 48)
            dve.wait_ge(S["norm"], 1)
            link(dve.scalar_tensor_tensor(out=reach[:, :], in0=vb_col[:, :], scalar=-1.0, in1=vb_col[:, :],
                                          op0=ALU.mult, op1=ALU.max))
            link(dve.scalar_tensor_tensor(out=reach[:, :], in0=norms[:, 0:1], scalar=float(np.sqrt(D)), in1=reach[:, :],
                                          op0=ALU.mult, op1=ALU.add))
            dve.tensor_tensor(reach[:, :], reach[:, :], norms[:, 1:2], ALU.mult).then_inc(S["reach_in"], 1)

            def fill_out(f):
                dve.wait_ge(S["fill_turned"], f + 1)
                dve.tensor_copy(xnT[:, (f - 1) * L:f * L], B(f)).then_inc(S["fill_out_v"], 1)

            fill_out(dve_fills[0])
            dve.wait_ge(S["reach"], 1)
            link(dve.tensor_scalar(sigma[:, :], B(7)[:, 0:1], 4.0, 1.0 / G_TOP, ALU.max, ALU.mult))
            mark(dve.tensor_scalar(scale_neg[:, :], sigma[:, :], -SCALE, None, ALU.mult))
            link(dve.reciprocal(sigma[:, :], sigma[:, :]))
            mark(dve.tensor_scalar(ub_row[:, :], ub_row[:, :], sigma[:, 0:1], None, ALU.mult))
            mark(dve.tensor_tensor(ub_col[:, :], ub_col[:, :], sigma[:, :], ALU.mult))
            mark(dve.tensor_tensor(vb_col[:, :], vb_col[:, :], sigma[:, :], ALU.mult))
            dve.wait_ge(S["fill_out_a"], 1)
            link(dve.tensor_scalar(wT[:, WQ * D:(WQ + 1) * D], wT[:, WQ * D:(WQ + 1) * D], sigma[:, 0:1], None, ALU.mult))
            dve.sem_inc(S["sigma"], 1)
            fill_out(dve_fills[1])
            def part3(n):
                dve.wait_ge(S["part2"], n + 1)
                dve.tensor_tensor(parts[:, n % 3, n // 3, 2, :], rests[n % 5], parts[:, n % 3, n // 3, 1, :],
                                  ALU.subtract).then_inc(S["part3_v"], 1)

            for n in range(3 * NB):
                b, kind = n // 3, n % 3
                dve.wait_ge(S["part1"], min(n + 2 if kind == 0 else n + 1, 3 * NB))
                if n >= 5:
                    after_part3(dve, n - 5)
                src = B(2 * b + (kind == 2))
                if kind < 2:
                    ins = dve.scalar_tensor_tensor(out=rests[n % 5], in0=src, scalar=(vb_col, ub_col)[kind][:, 0:1],
                                                   in1=parts[:, kind, b, 0, :], op0=ALU.add, op1=ALU.subtract)
                else:
                    ins = dve.tensor_tensor(rests[n % 5], src, parts[:, kind, b, 0, :], ALU.subtract)
                ins.then_inc(S["rest_ready"], 1)
                if n % 2 == 0 and n >= 4:
                    part3(n - 3)
            part3(3 * NB - 3)
            part3(3 * NB - 1)
            for t in range(T):
                dve.wait_ge(S["tokens_done"], t + 1)
                bank_t = B(2 + t % 6)
                dve.tensor_copy(q_u[:, t % 2, :], bank_t[:, 0:D]).then_inc(S["q_u"], 1)
                dve.wait_ge(S["q_u"], t + 1)
                dve.tensor_tensor(prod0[:, t, :], bank_t[:, 2 * D:3 * D], q_u[:, t % 2, :], ALU.mult).then_inc(S["next_product"], 1)
            dve.wait_ge(S["next_product"], T)
            link(dve.tensor_reduce(s_next, prod0.rearrange("p t (h d) -> p (t h) d", d=DH), AX.X, ALU.add))
            dve.wait_ge(in_small, 16)
            link(dve.tensor_scalar(s_next, s_next, scale_neg[:, 0:1], None, ALU.mult))
            link(dve.memset(neg_s[:, H, :], 0.0))
            link(dve.tensor_tensor(neg_s[:, 0:H, :].rearrange("p h t -> p t h"),
                                   s_next.rearrange("p (t h) -> p t h", h=H),
                                   last_key.unsqueeze(2).to_broadcast([P, T, H]), ALU.add))
            link(dve.tensor_copy(start[:, 0:T // 2], neg_s[:, 0, 0:T // 2]))

            def rotate(n, half, first):
                dve.wait_ge(S["g_done"], n + 1)
                if not first:
                    dve.wait_ge(S["g_ready"], n - 1)
                dve.tensor_tensor(turned_g[:, half, :], B(6), rot[:, half, :], ALU.mult).then_inc(S["g_rot"], 1)

            def hidden_gate(j):
                if j >= 3:
                    dve.wait_ge(S["hidden_ready"], j - 2)
                dve.wait_ge(S["gate_tanh"], j + 1)
                dve.scalar_tensor_tensor(out=hg[j % 3], in0=th[:, j % 3, :], scalar=1.0, in1=B(2 * (j % 3)),
                                         op0=ALU.add, op1=ALU.mult).then_inc(S["hidden_gate"], 1)

            def hidden_up(j):
                b = j // 3
                if b >= 2:
                    dve.wait_ge(S["down_done"], b - 1)
                dve.wait_ge(S["hidden_gate"], j + 1)
                dve.tensor_tensor(hidden[b % 2][:, j % 3, :], B(2 * (j % 3) + 1), hg[j % 3], ALU.mult).then_inc(S["hidden_ready"], 1)

            def ffn_out(b):
                dve.wait_ge(S["out_tanh"], b + 1)
                dve.scalar_tensor_tensor(out=ffn[:, 4 * b:4 * b + 4, :].rearrange("p t c -> p (t c)"), in0=th2[:, b % 2, :],
                                         scalar=1.0, in1=B(7), op0=ALU.add, op1=ALU.mult).then_inc(S["ffn_ready"], 1)

            dve.wait_ge(S["part3_p"], 3 * NB // 2)
            dve.wait_ge(S["part3_v"], 3 * NB // 2)
            for j in range(3 * NB):
                hidden_gate(j)
                hidden_up(j)
                if j >= 6 and j % 3 == 0:
                    ffn_out(j // 3 - 2)
                if j in (9, 10):
                    if j == 9:
                        dve.wait_ge(in_tab, 48)
                        dve.wait_ge(ldqv[0], 48)
                    rotate(j - 9, j - 9, True)
            ffn_out(NB - 2)
            ffn_out(NB - 1)
            dve.wait_ge(S["v_moved"], 48)
            dve.wait_ge(S["v_split"], NB)

            def o_evacuate(h, b, n):
                dve.wait_ge(S["sums_done"], 4 * n + 4)
                dst = o_all[:, 4 * b:4 * b + 4, h, :] if isinstance(h, int) else o_all[:, 4 * b:4 * b + 4, bass.ds(h, 1), :]
                src = B(7)[:, 0:4 * VW].rearrange("p (i s d) -> p i d s", i=4, s=SPLITS)
                if not isinstance(h, int):
                    dst = dst.rearrange("p i a d -> p i (a d)")
                dve.tensor_reduce(dst, src, AX.X, ALU.add).then_inc(S["sums_out"], 1)

            def low_half(U, u):
                dve.wait_ge(S["hi_done"], U + 1)
                dve.scalar_tensor_tensor(out=probT[:, u % 4, 1, :], in0=B(4 + u % 2), scalar=P_TOP, in1=probT[:, u % 4, 0, :],
                                         op0=ALU.mult, op1=ALU.subtract).then_inc(S["low_done"], 1)

            def head(h, first, last):
                for b in range(NB):
                    for i in range(TPB):
                        u = 4 * b + i
                        U = h * 16 + u
                        par = u % 2
                        if i in (0, 2) and not (last and b == NB - 1):
                            rotate(h * 8 + 2 * (b + 1) + i // 2, i // 2, False)
                        if i == V_LAG % TPB and not (first and b < 2):
                            if b >= 2:
                                o_evacuate(h, b - 2, h * 4 + b - 2)
                            else:
                                o_evacuate(h - 1, b + 2, h * 4 + b - 2)
                        if not (first and u < LOW_LAG):
                            low_half(U - LOW_LAG, (u - LOW_LAG) % 4)
                        dve.wait_ge(S["scored"], U + 1)
                        if not (first and u < 4):
                            dve.wait_ge(S["exped"], U - 3)
                        dve.memset(pace[:, par:par + 1], 0.0)
                        dve.tensor_tensor_reduce(s_sb[:, i, :], bank[par][:, :, :].rearrange("p a c -> p (a c)")[:, 0:WIDE],
                                                 mask[:, i, :], scale_neg[:, 0:1], start[:, u:u + 1], ALU.add, ALU.min,
                                                 shift_now[:, u:u + 1]).then_inc(S["maxed"], 1)

            head(0, True, False)
            with dve.Fori(1, H - 1) as h:
                head(h, False, False)
            head(H - 1, False, True)
            for back in range(LOW_LAG, 0, -1):
                if back == TPB - 1:
                    o_evacuate(H - 1, NB - 2, H * 4 - 2)
                low_half(H * 16 - back, -back % 4)
            o_evacuate(H - 1, NB - 1, H * 4 - 1)
            link(dve.tensor_tensor(e1d, shift[:, :, :].rearrange("p h t -> p (h t)"),
                                   neg_s[:, 0:H, :].rearrange("p h t -> p (h t)"), ALU.subtract))
            dve.sem_inc(S["e1_in"], 1)
            dve.wait_ge(S["e1"], 2)
            dve.wait_ge(S["sums_out"], NB * H)
            link(dve.tensor_tensor(den, o_all[:, :, :, DH], e1.rearrange("p (h t) -> p t h", h=H), ALU.add))
            dve.reciprocal(den, den).then_inc(S["den"], 1)
            dve.wait_ge(S["den"], 1)

            def heads(a):
                return a.rearrange("p n (h d) -> p n h d", h=H)

            def result0(pair, between=None):
                g = pair[0] >= 2
                k = {}
                for i in pair if g == 0 else ():
                    k[i] = mark(dve.tensor_tensor(heads(group(ffn, i)), heads(group(ffn, i)),
                                                  group(den, i).unsqueeze(3).to_broadcast([P, NB, H, DH]), ALU.mult))
                j = {}
                for i in pair:
                    dve.wait_ge(S["next_share"], i + 1)
                    j[i] = mark(dve.tensor_tensor(heads(num[:, i]), heads(num[:, i]), group(o_all, i)[:, :, :, 0:DH], ALU.add))
                if between:
                    between()
                for i in pair:
                    if g:
                        dve.wait_ge(S["gate_over"], i - 1)
                    after(j[i])
                    j[i] = mark(dve.tensor_tensor(num[:, i], num[:, i], group(ffn, i), ALU.mult))
                for i in pair:
                    after(j[i])
                    j[i] = mark(dve.scalar_tensor_tensor(out=group(x, i), in0=num[:, i], scalar=DEQ ** 3 / 4,
                                                         in1=group(x, i), op0=ALU.mult, op1=ALU.add))
                s_at = {}
                for i in pair:
                    after(j[i])
                    for t in range(i, T, TPB):
                        s_at[t] = mark(dve.bn_stats(stats[:, t, :], x[:, t, :]))
                for i in pair:
                    for t in range(i, T, TPB):
                        after(s_at[t])
                        ins = dve.bn_aggr(mean_var[:, t, :], stats[:, t, :])
                        last = mark(ins)
                after(last)
                dve.sem_inc(S["x2_ready"], 1)

            def norm_factors(g):
                dve.wait_ge(S["deviation1"], g + 1)
                both = slice(g, g + 1 if g < 2 else TPB)
                r, m, o = (a.rearrange("p (n i) -> p n i", i=TPB)[:, :, both]
                           for a in (rstd[:, :], mean_var[:, :, 0], offset[:, :]))
                link(dve.reciprocal(r, r))
                dve.scalar_tensor_tensor(out=o, in0=m, scalar=-1.0, in1=r, op0=ALU.mult, op1=ALU.mult).then_inc(S["norm_factors"], 1)

            def router(i):
                dve.wait_ge(S["qkv_out"], NB * (i + 1))
                lo = group(qkv, i)[:, :, 3 * D:]
                a = mark(dve.tensor_reduce(rsum[:, i], lo, AX.X, ALU.max))
                g4 = gt.rearrange("p t (e f) -> p t e f", e=E_CNT)
                q4 = eq.rearrange("p t (e f) -> p t e f", e=E_CNT)
                other = lo.unsqueeze(2).to_broadcast([P, NB, E_CNT, E_CNT])
                own = lo.unsqueeze(3).to_broadcast([P, NB, E_CNT, E_CNT])
                q = mark(dve.tensor_tensor(q4, other, own, ALU.is_equal))
                after(a)
                dve.tensor_tensor(lg[:, i], lo, rsum[:, i].unsqueeze(2).to_broadcast([P, NB, E_CNT]), ALU.subtract)\
                    .then_inc(S["logits_shifted"], 1)
                g = mark(dve.tensor_tensor(g4, other, own, ALU.is_gt))
                after(q)
                q = mark(dve.tensor_tensor(eq, eq, tri.unsqueeze(1).to_broadcast([P, NB, E_CNT * E_CNT]), ALU.mult))
                dve.wait_ge(S["logits_exp"], i + 1)
                a = mark(dve.tensor_reduce(rsum[:, i], lg[:, i], AX.X, ALU.add))
                after(q)
                g = mark(dve.tensor_tensor(gt, gt, eq, ALU.add))
                after(a)
                a = mark(dve.reciprocal(rsum[:, i], rsum[:, i]))
                after(g)
                g = mark(dve.tensor_reduce(rank[:, i].rearrange("p (t e) -> p t e", e=E_CNT), g4, AX.X, ALU.add))
                after(a)
                a = mark(dve.tensor_tensor(lg[:, i], lg[:, i], rsum[:, i].unsqueeze(2).to_broadcast([P, NB, E_CNT]), ALU.mult))
                after(a)
                dve.scalar_tensor_tensor(out=gate[:, i].rearrange("p t e -> p (t e)"), in0=rank[:, i],
                                         scalar=TOPK - 0.5, in1=lg[:, i].rearrange("p t e -> p (t e)"),
                                         op0=ALU.is_lt, op1=ALU.mult).then_inc(S["gate"], 1)

            def over_batches(a):
                return a.rearrange("p n (m h) -> p n h m", m=NB)

            def score_sums(k, i):
                link(qk_product(dve, k, i, NB - QK_DVE, NB))
                dve.wait_ge(S["product"], k + 1)
                ins = dve.tensor_reduce(sc[:, i].rearrange("p n x -> p (n x)"),
                                        products[k % 2].rearrange("p (a d) -> p a d", d=DH), AX.X, ALU.add)
                ins.then_inc(S["product_used"], 1)
                dve.wait_ge(S["product_used"], k + 1)
                m = smax[:, i].rearrange("p (n h) -> p n h", n=NB)
                link(dve.tensor_reduce(m, over_batches(sc[:, i]), AX.X, ALU.max))
                four = sc[:, i].rearrange("p n (m h) -> p n m h", m=NB)
                dve.tensor_tensor(four, four, m.unsqueeze(2).to_broadcast([P, NB, NB, H]), ALU.subtract).then_inc(S["scores1_shifted"], 1)

            def probabilities(i):
                dve.wait_ge(S["scores1_exp"], i + 1)
                m = ssum[:, i].rearrange("p (n h) -> p n h", n=NB)
                link(dve.tensor_reduce(m, over_batches(pr[:, i]), AX.X, ALU.add))
                link(dve.reciprocal(m, m))
                four = pr[:, i].rearrange("p n (m h) -> p n m h", m=NB)
                dve.tensor_tensor(four, four, m.unsqueeze(2).to_broadcast([P, NB, NB, H]), ALU.mult).then_inc(S["probs"], 1)

            def value_sums(k, i):
                dve.wait_ge(S["probs"], i + 1)
                for n in range(NB - PV_DVE, NB):
                    p = mark(pv_product(dve, k, i, n))
                after(p)
                dve.wait_ge(S["product"], k + 1)
                dve.tensor_reduce(group(attn, i), products[k % 2].rearrange("p (n m c) -> p n c m", n=NB, m=NB),
                                  AX.X, ALU.add).then_inc(S["product_used"], 1)

            def experts(i, tiles):
                step = {}
                for e in range(MOE_DVE):
                    for n in tiles:
                        k = NB * i + n
                        m = moe[:, TPB * n + i, :]
                        src = moe_bank(k)[:, 0, e * D:(e + 1) * D]
                        if e == 0:
                            dve.wait_ge(S["experts_done"], k + 1)
                            ins = dve.tensor_scalar(m, src, gate[:, i, n, 0:1], None, ALU.mult)
                        else:
                            after(step[n])
                            ins = dve.scalar_tensor_tensor(out=m, in0=src, scalar=gate[:, i, n, e:e + 1], in1=m,
                                                           op0=ALU.mult, op1=ALU.add)
                        if e < MOE_DVE - 1:
                            step[n] = mark(ins)
                        else:
                            ins.then_inc(S["moe_own"], 1)

            def result1(i):
                dve.wait_ge(S["moe_tanh"], i + 1)
                m = group(moe, i)
                link(dve.scalar_tensor_tensor(out=m, in0=th_moe[:, i, :].rearrange("p (n c) -> p n c", n=NB), scalar=1.0,
                                              in1=m, op0=ALU.add, op1=ALU.mult))
                dve.wait_ge(S["attn_projected"], i + 1)
                link(dve.scalar_tensor_tensor(out=m, in0=B(1).rearrange("p (n c) -> p n c", n=NB), scalar=0.5,
                                              in1=m, op0=ALU.mult, op1=ALU.mult))
                dve.tensor_tensor(group(x, i), group(x, i), m, ALU.add).then_inc(S["result_ready"], 1)

            result0((0,))
            result0((1,), lambda: norm_factors(0))
            result0((2, 3), lambda: norm_factors(1))
            norm_factors(2)
            first, second = (0, 1), (2, 3)
            router(0)
            score_sums(0, 0)
            router(1)
            probabilities(0)
            score_sums(1, 1)
            experts(0, first)
            probabilities(1)
            value_sums(2, 0)
            experts(0, second)
            router(2)
            score_sums(3, 2)
            experts(1, first)
            probabilities(2)
            value_sums(4, 1)
            experts(1, second)
            result1(0)
            router(3)
            score_sums(5, 3)
            experts(2, first)
            probabilities(3)
            value_sums(6, 2)
            experts(2, second)
            result1(1)
            experts(3, first)
            value_sums(7, 3)
            experts(3, second)
            result1(2)
            result1(3)

        @block.tensor
        def _(pe):
            pe.wait_ge(in_small, 16)
            pe.wait_ge(in_w0, 64)
            pe.wait_ge(S["ints_cast"], 1)
            for f in range(FILLS):
                if f:
                    pe.wait_ge(S["xn_ready"], 4 * f)
                for j in range(4):
                    src = xn[:, 4 * (f - 1) + j, :] if f else w_nat[:, j, :]
                    ins = pe.transpose(B(f)[:, j * P:(j + 1) * P], src, ident)
                ins.then_inc(S["fill_turned"], 1)
                if f == 1:
                    pe.wait_ge(S["reach_in"], 1)
                    pe.wait_ge(S["preset"], 7)
                    pe.matmul(B(7)[:, 0:1], ones[:, :], reach[:, :], start=True, stop=True).then_inc(S["reach"], 1)
            pe.wait_ge(S["sigma"], 1)
            for b in range(NB):
                for blk, bk in ((WQ, 0), (WK, 1)):
                    f = 2 * b + bk
                    if f < FILLS:
                        after_fill(pe, f)
                    after_fill(pe, b + 1)
                    pe.matmul(B(f), wT[:, blk * D:(blk + 1) * D], xnT[:, b * L:(b + 1) * L],
                              start=True, stop=True).then_inc(S["projected"], 1)

            def turn_weights(k, b8):
                for j in range(4):
                    ins = pe.transpose(b8[:, j * P:(j + 1) * P], w_nat[:, 4 * (k + 1) + j, :], ident)
                ins.then_inc(S["weights_turned"], 1)

            pe.wait_ge(S["ints_cast"], 3)
            for k in range(2):
                pe.wait_ge(S["rest_ready"], 2 + k)
                turn_weights(k, B(k))
            for t in range(T):
                b8 = B(2 + t % 6)
                if t < 6:
                    pe.wait_ge(S["rest_ready"], (5, 6, 8, 9, 11, 12)[t])
                else:
                    pe.wait_ge(S["v_out"], t - 5)
                pe.matmul(b8[:, 0:D], ones[0:1, :], ub_row[0:1, :], start=True, stop=False)
                pe.matmul(b8[:, 0:D], xnT[:, t * P:(t + 1) * P], wT[:, WQ * D:(WQ + 1) * D], start=False, stop=True)
                pe.matmul(b8[:, D:2 * D], xnT[:, t * P:(t + 1) * P], wT[:, WV * D:(WV + 1) * D], start=True, stop=True)
                pe.matmul(b8[:, 2 * D:3 * D], xnT[:, t * P + 1:(t + 1) * P + 1], wT[:, WK * D:(WK + 1) * D],
                          start=True, stop=True).then_inc(S["tokens_done"], 1)
            pe.wait_ge(in_w1, 80)
            for k in range(2, 5):
                if k == 4:
                    pe.wait_ge(S["weights_out"], 3)
                else:
                    pe.wait_ge(S["v_out"], 10 + k + 1)
                turn_weights(k, B(6 + k % 2))

            def turn(n, h, par, half, first):
                if not first:
                    pe.wait_ge(S["g_rot"], n)
                cols = slice(half * 256, half * 256 + 256)
                wr = wr_st[:, h, :] if isinstance(h, int) else wr_st[:, bass.ds(h, 1), :].rearrange("p a n -> p (a n)")
                pe.matmul(B(6)[:, 0:256], wr[:, 0:D], qv_st[:, par, cols], start=True, stop=True)
                pe.matmul(B(6)[:, 256:512], wr[:, D:2 * D], qv_st[:, par, cols], start=True, stop=True)\
                    .then_inc(S["g_done"], 1)

            def gate_up(j):
                b, k = j // 3, j % 3
                if j >= 3:
                    pe.wait_ge(S["hidden_ready"], j - 2)
                for which, blk in ((0, k), (1, 3 + k)):
                    for part in range(2):
                        ins = pe.matmul(B(2 * k + which), w16[:, blk * D:(blk + 1) * D], x16[:, part, b * L:(b + 1) * L],
                                        start=(part == 0), stop=(part == 1))
                ins.then_inc(S["gate_up_done"], 1)

            def down(b):
                pe.wait_ge(S["hidden_ready"], 3 * b + 3)
                if b >= 1:
                    pe.wait_ge(S["ffn_ready"], b)
                for i in range(TPB):
                    for k in range(3):
                        ins = pe.matmul(B(7)[:, i * P:(i + 1) * P], hidden[b % 2][:, k, i * P:(i + 1) * P],
                                        wT[:, (WD + k) * D:(WD + k + 1) * D], start=(k == 0), stop=(k == 2))
                ins.then_inc(S["down_done"], 1)

            pe.wait_ge(S["w16"], 1)
            pe.wait_ge(S["x_low"], NB)
            pe.wait_ge(S["v_out"], T)
            pe.wait_ge(S["weights_out"], 5)
            for j in range(3 * NB):
                gate_up(j)
                if j >= 5 and j % 3 == 2:
                    down(j // 3 - 1)
                if j == 9:
                    pe.wait_ge(in_tab, 48)
                    pe.wait_ge(ld_wr, 48)
                    pe.wait_ge(ldqv[0], 48)
                    turn(0, 0, 0, 0, True)
                if j == 11:
                    turn(1, 0, 0, 1, False)
            down(NB - 1)
            pe.wait_ge(ldqv[1], 48)
            turn(2, 0, 1, 0, False)

            def scores(U, par, spar, i, first):
                if not first:
                    pe.wait_ge(S["maxed"], U - 1)
                main, extra = bank[par][:, 0, :], bank[par][:, 1, 0:P]
                qu = qu_st[:, spar, i * P:(i + 1) * P]
                pe.matmul(main, qu, k_st[:, spar, :], start=True, stop=False)
                pe.matmul(extra, qu, k_st[:, spar, i * P:(i + 1) * P], start=True, stop=False)
                edge = (i + 1) * P
                for n, (pg, pw) in enumerate(((0, 0), (0, 1), (1, 0))):
                    g_low = g_sb[:, spar, pg, i * P:(i + 1) * P]
                    g_up = g_sb[:, spar, pg, i * P + 1:(i + 1) * P + 1]
                    done = n == 2
                    pe.matmul(main[:, 0:edge], g_low, waves[:, 0, pw, 0:edge], start=False, stop=(done and edge == L))
                    if edge < L:
                        pe.matmul(main[:, edge:L], g_up, waves[:, 1, pw, edge:L], start=False, stop=done)
                    ins = pe.matmul(extra, g_up, waves[:, 1, pw, i * P:edge], start=False, stop=done)
                ins.then_inc(S["scored"], 1)

            def transpose(U, par, i, first):
                pe.wait_ge(S["merged"], U + 1)
                if not first:
                    pe.wait_ge(S["low_done"], U - 1)
                for c in range(TPB):
                    ins = pe.transpose(B(4 + par)[:, c * P:(c + 1) * P], prob[:, i, c * P:(c + 1) * P], ident)
                ins.then_inc(S["turned"], 1)

            def values(U, h, u, n, first):
                b, i = u // 4, u % 4
                pe.wait_ge(S["low_done"], U + 1)
                if i == 0 and not first:
                    pe.wait_ge(S["sums_out"], n)
                for c in range(TPB):
                    if isinstance(h, int):
                        v = v_parts[:, 4 * b + c, h, :]
                    else:
                        v = v_parts[:, 4 * b + c, bass.ds(h, 1), :].rearrange("p a d -> p (a d)")
                    for half in range(2):
                        ins = pe.matmul(B(7)[:, i * VW:(i + 1) * VW], probT[:, i, half, c * P:(c + 1) * P], v,
                                        start=(c == 0 and half == 0), stop=(c == TPB - 1 and half == 1))
                ins.then_inc(S["sums_done"], 1)

            def head(h, first, last):
                for b in range(NB):
                    for i in range(TPB):
                        u = 4 * b + i
                        U = h * 16 + u
                        if i == 0:
                            pe.wait_ge(S["g_ready"], h * 8 + 2 * b + 2)
                            pe.wait_ge(ld[b % 2], 96 * (2 * h + b // 2 + 1))
                        scores(U, u % 2, b % 2, i, first and u < 2)
                        ahead = {1: 1, 3: 2}.get(i)
                        if ahead and not (last and b + ahead >= NB):
                            nb, nh = ((b + ahead) % NB, h + (b + ahead) // NB)
                            if i == 3:
                                pe.wait_ge(ldqv[nb % 2], 48 * (2 * nh + nb // 2 + 1))
                            turn(h * 8 + 2 * (b + ahead) + (i == 1), nh, nb % 2, int(i == 1), False)
                        if not (first and u < T_LAG):
                            transpose(U - T_LAG, (u - T_LAG) % 2, (u - T_LAG) % 4, first and u < T_LAG + 2)
                        if first and u == V_LAG:
                            pe.wait_ge(S["ffn_ready"], NB)
                        if u >= V_LAG:
                            values(U - V_LAG, h, u - V_LAG, h * 4 + (u - V_LAG) // 4, first and u < V_LAG + 4)
                        elif not first:
                            values(U - V_LAG, h - 1, 16 - V_LAG + u, h * 4 - 1 - (V_LAG - 1 - u) // 4, False)

            pe.wait_ge(S["preset"], 8)
            head(0, True, False)
            with pe.Fori(1, H - 1) as h:
                head(h, False, False)
            head(H - 1, False, True)
            U = H * 16
            for k in range(V_LAG):
                u = 16 + k - V_LAG
                values(U + k - V_LAG, H - 1, u, (H - 1) * 4 + u // 4, False)
                if k < T_LAG:
                    transpose(U + k - T_LAG, (k - T_LAG) % 2, (k - T_LAG) % 4, False)
            pe.wait_ge(S["maxed"], H * 16)
            for n in range(2):
                for j in range(4):
                    e = 4 * n + j
                    ins = pe.matmul(B(n)[:, j * D:(j + 1) * D], wT[:, (WI + e) * D:(WI + e + 1) * D], wo1[:, e, :],
                                    start=True, stop=True)
                ins.then_inc(S["expert_weights"], 1)

            def turn_xn(i):
                pe.wait_ge(S["xn1_ready"], NB * i + NB)
                if i < 2:
                    pe.wait_ge(S["expert_weights_out"], i + 1)
                else:
                    pe.wait_ge(S["xn1_out"], i - 1)
                for n in range(NB):
                    ins = pe.transpose(B(i % 2)[:, n * P:(n + 1) * P], xn[:, TPB * n + i, :], ident)
                ins.then_inc(S["xn1_turned"], 1)

            def project(i):
                pe.wait_ge(S["xn1_out"], i + 1)
                for n in range(NB):
                    k = NB * i + n
                    t = TPB * n + i
                    if k >= 2:
                        pe.wait_ge(S["qkv_out"], k - 1)
                    pe.matmul(B(2 + k % 2)[:, 0:QKVR], ones_rows, bias_rows[:, 0:QKVR], start=True, stop=False)
                    pe.matmul(B(2 + k % 2)[:, 0:QKVR], xnT[:, t * P:(t + 1) * P], wT[:, WQKV * D:], start=False, stop=True)\
                        .then_inc(S["qkv_done"], 1)

            def every_expert(i, tiles):
                for n in tiles:
                    k = NB * i + n
                    t = TPB * n + i
                    if k >= 3:
                        pe.wait_ge(S["moe_own"], k - 2)
                        pe.wait_ge(S["experts_gated"], k - 2)
                    for a in range(2):
                        ins = pe.matmul(moe_bank(k)[:, a, :], xnT[:, t * P:(t + 1) * P],
                                        wc[:, 4 * a:4 * a + 4, :].rearrange("p e c -> p (e c)"), start=True, stop=True)
                    ins.then_inc(S["experts_done"], 1)

            def turn_attn(i, k):
                pe.wait_ge(S["product_used"], k + 1)
                if i >= 1:
                    pe.wait_ge(S["attn_turned_out"], i)
                for n in range(NB):
                    ins = pe.transpose(B(0)[:, n * P:(n + 1) * P], attn[:, TPB * n + i, :], ident)
                ins.then_inc(S["attn_turned"], 1)

            def project_attn(i):
                pe.wait_ge(S["attn_turned_out"], i + 1)
                if i >= 1:
                    pe.wait_ge(S["result_ready"], i)
                for n in range(NB):
                    dst = B(1)[:, n * D:(n + 1) * D]
                    pe.matmul(dst, ones_rows, bias_rows[:, QKVR:], start=True, stop=False)
                    ins = pe.matmul(dst, attnT[:, i * L + n * P:i * L + (n + 1) * P], wT[:, WP * D:(WP + 1) * D],
                                    start=False, stop=True)
                ins.then_inc(S["attn_projected"], 1)

            pe.wait_ge(in_w1, 80)
            pe.wait_ge(S["bias_rows"], 1)
            turn_xn(0)
            project(0)
            turn_xn(1)
            project(1)
            turn_xn(2)
            turn_xn(3)
            project(2)
            project(3)
            pe.wait_ge(S["low_done"], H * 16)
            pe.wait_ge(S["sums_out"], H * NB)
            pe.wait_ge(S["qkv_out"], T)
            first, second = (0, 1), (2, 3)
            every_expert(0, first)
            every_expert(0, second)
            every_expert(1, first[0:1])
            turn_attn(0, 2)
            project_attn(0)
            every_expert(1, first[1:])
            every_expert(1, second)
            every_expert(2, first[0:1])
            turn_attn(1, 4)
            project_attn(1)
            every_expert(2, first[1:])
            every_expert(2, second)
            every_expert(3, first[0:1])
            turn_attn(2, 6)
            project_attn(2)
            every_expert(3, first[1:])
            every_expert(3, second)
            turn_attn(3, 7)
            project_attn(3)


_INS = ["L0_attn_w", "L0_attn_Wq", "L0_attn_Wk", "L0_attn_Wv", "L0_attn_Wr", "L0_attn_u_bias", "L0_attn_v_bias",
        "L0_ffn_w_gate", "L0_ffn_w_up", "L0_ffn_w_down", "L1_attn_Wqkv", "L1_attn_bqkv", "L1_attn_Wproj",
        "L1_attn_bproj", "L1_ffn_Wr", "L1_ffn_Wi", "L1_ffn_Wo"]


def kernel(**inputs):
    import numpy as _np
    import concourse.bacc as _bacc
    from concourse import mybir as _mybir
    from concourse.bass_utils import run_bass_kernel_spmd as _run

    nc = _bacc.Bacc("TRN2", target_bir_lowering=False, num_devices=1)
    arrays, args = {}, []
    for name, a in [(n, inputs[n]) for n in _INS] + list(tables().items()):
        a = _np.ascontiguousarray(a)
        arrays[f"in_{name}"] = a
        args.append(nc.dram_tensor(f"in_{name}", a.shape, _mybir.dt.from_np(a.dtype), kind="ExternalInput").ap())
    out = nc.dram_tensor("out", (NB, L, D), _mybir.dt.float32, kind="ExternalOutput").ap()
    build(nc, *args, out)
    r = _run(nc, [arrays], core_ids=[0])
    return r.results[0]["out"]
```
